# Optimizing a Trainium2 kernel written in Bass

```python
import numpy as np
import jax
import jax.numpy as jnp

def _softmax(x, axis=-1):
    return jax.nn.softmax(x, axis=axis)
def _gelu(x):
    return jax.nn.gelu(x, approximate=True)
def _silu(x):
    return jax.nn.silu(x)
def _sigmoid(x):
    return jax.nn.sigmoid(x)
def _layernorm(x, axis=-1, eps=1e-5):
    m = jnp.mean(x, axis=axis, keepdims=True)
    v = jnp.var(x, axis=axis, keepdims=True)
    return (x - m) / jnp.sqrt(v + eps)
def _scatter_add(tgt, idx, src, axis=0):
    return tgt.at[idx].add(src)
def _segment_sum(src, seg, n):
    return jax.ops.segment_sum(src, seg, n)

kernel_name = 'mk_conv_seq_d1_conv_nhwc128_465bcd'

def setup_inputs(seed: int = 0):
    np.random.seed(seed)
    _w = jnp.asarray
    def _rec_inputs():
        import jax
        import jax.numpy as jnp
        _gk = jax.random.key(seed)
        x = -0.0003929 + 0.9999 * jax.random.normal(jax.random.fold_in(_gk, 1), (16, 64, 128, 128), jnp.float32)
        return x
    x = _rec_inputs()
    def _L0_conv_setup():
        import jax, jax.numpy as jnp
        import numpy as np
        B, R, K, M = (16, 64, 128, 128)
        H, D = (8, 16)
        FF = 512
        EPS = 1e-05

        def _layernorm(x, g, b):
            mu = jnp.mean(x, axis=-1, keepdims=True)
            var = jnp.mean(jnp.square(x - mu), axis=-1, keepdims=True)
            return (x - mu) * jax.lax.rsqrt(var + EPS) * g + b
        key = jax.random.key(seed)
        ks = jax.random.split(key, 16)
        s = 1.0 / np.sqrt(M)
        sf = 1.0 / np.sqrt(FF)
        return {'route': jax.random.normal(ks[0], (B, R, K, M), dtype=jnp.float32), 'wq': jax.random.uniform(ks[1], (M, M), jnp.float32, -s, s), 'bq': jax.random.uniform(ks[2], (M,), jnp.float32, -s, s), 'wk': jax.random.uniform(ks[3], (M, M), jnp.float32, -s, s), 'bk': jax.random.uniform(ks[4], (M,), jnp.float32, -s, s), 'wv': jax.random.uniform(ks[5], (M, M), jnp.float32, -s, s), 'bv': jax.random.uniform(ks[6], (M,), jnp.float32, -s, s), 'wo': jax.random.uniform(ks[7], (M, M), jnp.float32, -s, s), 'bo': jax.random.uniform(ks[8], (M,), jnp.float32, -s, s), 'w1': jax.random.uniform(ks[9], (M, FF), jnp.float32, -s, s), 'b1': jax.random.uniform(ks[10], (FF,), jnp.float32, -s, s), 'w2': jax.random.uniform(ks[11], (FF, M), jnp.float32, -sf, sf), 'b2': jax.random.uniform(ks[12], (M,), jnp.float32, -sf, sf), 'ln1_g': jnp.ones((M,), jnp.float32), 'ln1_b': jnp.zeros((M,), jnp.float32), 'ln2_g': jnp.ones((M,), jnp.float32), 'ln2_b': jnp.zeros((M,), jnp.float32)}
    _L0_conv_all = _L0_conv_setup()
    _L0_conv_in = {k: v for k, v in _L0_conv_all.items() if k in ('wq', 'bq', 'wk', 'bk', 'wv', 'bv', 'wo', 'bo', 'w1', 'b1', 'w2', 'b2', 'ln1_g', 'ln1_b', 'ln2_g', 'ln2_b', )}
    del _L0_conv_all

    return {
        "x": x,
        "L0_conv_wq": _L0_conv_in["wq"],
        "L0_conv_bq": _L0_conv_in["bq"],
        "L0_conv_wk": _L0_conv_in["wk"],
        "L0_conv_bk": _L0_conv_in["bk"],
        "L0_conv_wv": _L0_conv_in["wv"],
        "L0_conv_bv": _L0_conv_in["bv"],
        "L0_conv_wo": _L0_conv_in["wo"],
        "L0_conv_bo": _L0_conv_in["bo"],
        "L0_conv_w1": _L0_conv_in["w1"],
        "L0_conv_b1": _L0_conv_in["b1"],
        "L0_conv_w2": _L0_conv_in["w2"],
        "L0_conv_b2": _L0_conv_in["b2"],
        "L0_conv_ln1_g": _L0_conv_in["ln1_g"],
        "L0_conv_ln1_b": _L0_conv_in["ln1_b"],
        "L0_conv_ln2_g": _L0_conv_in["ln2_g"],
        "L0_conv_ln2_b": _L0_conv_in["ln2_b"],
    }

def reference(x, L0_conv_wq, L0_conv_bq, L0_conv_wk, L0_conv_bk, L0_conv_wv, L0_conv_bv, L0_conv_wo, L0_conv_bo, L0_conv_w1, L0_conv_b1, L0_conv_w2, L0_conv_b2, L0_conv_ln1_g, L0_conv_ln1_b, L0_conv_ln2_g, L0_conv_ln2_b):
    import jax
    import jax.numpy as jnp
    def _L0_conv_ref(route, wq, bq, wk, bk, wv, bv, wo, bo, w1, b1, w2, b2, ln1_g, ln1_b, ln2_g, ln2_b):
        import jax, jax.numpy as jnp
        import numpy as np
        B, R, K, M = (16, 64, 128, 128)
        H, D = (8, 16)
        FF = 512
        EPS = 1e-05

        def _layernorm(x, g, b):
            mu = jnp.mean(x, axis=-1, keepdims=True)
            var = jnp.mean(jnp.square(x - mu), axis=-1, keepdims=True)
            return (x - mu) * jax.lax.rsqrt(var + EPS) * g + b
        b_, r_, k_, m_ = route.shape
        q = (route @ wq + bq).reshape(b_, r_, k_, H, D)
        k = (route @ wk + bk).reshape(b_, r_, k_, H, D)
        v = (route @ wv + bv).reshape(b_, r_, k_, H, D)
        scores = jnp.einsum('brkhd,brnhd->brknh', q, k) / D ** 0.5
        attn = jax.nn.softmax(scores, axis=3)
        out = jnp.einsum('brknh,brnhd->brkhd', attn, v).reshape(b_, r_, k_, m_)
        out = out @ wo + bo
        x = _layernorm(route + out, ln1_g, ln1_b)
        ff = jax.nn.relu(x @ w1 + b1) @ w2 + b2
        return _layernorm(x + ff, ln2_g, ln2_b)

    def _gn(v, G=32, eps=1e-5):
        B_, H_, W_, C_ = v.shape
        g = v.reshape(B_, H_, W_, G, C_ // G)
        m = jnp.mean(g, axis=(1, 2, 4), keepdims=True)
        s = jnp.var(g, axis=(1, 2, 4), keepdims=True)
        return ((g - m) / jnp.sqrt(s + eps)).reshape(v.shape)

    def _ln_c(v, eps=1e-6):
        m = jnp.mean(v, axis=-1, keepdims=True)
        s = jnp.var(v, axis=-1, keepdims=True)
        return (v - m) / jnp.sqrt(s + eps)

    def _ln_t(v, eps=1e-5):
        m = jnp.mean(v, axis=-1, keepdims=True)
        s = jnp.var(v, axis=-1, keepdims=True)
        return (v - m) / jnp.sqrt(s + eps)

    def _to_tokens(v):
        B_, H_, W_, C_ = v.shape
        return v.reshape(B_, H_ * W_, C_)
    def _from_tokens(t, like):
        return t.reshape(like.shape)

    x = _L0_conv_ref(x, L0_conv_wq, L0_conv_bq, L0_conv_wk, L0_conv_bk, L0_conv_wv, L0_conv_bv, L0_conv_wo, L0_conv_bo, L0_conv_w1, L0_conv_b1, L0_conv_w2, L0_conv_b2, L0_conv_ln1_g, L0_conv_ln1_b, L0_conv_ln2_g, L0_conv_ln2_b)
    return x


_drawn_inputs = setup_inputs


def setup_inputs(seed=0):
    import zlib

    import numpy as np

    out = dict(_drawn_inputs(seed))
    spreads = {'L0_conv_ln1_g': (1.0, 0.2),
     'L0_conv_ln1_b': (0.0, 0.1),
     'L0_conv_ln2_g': (1.0, 0.2),
     'L0_conv_ln2_b': (0.0, 0.1)}
    factors = {'L0_conv_wq': 3.992,
     'L0_conv_bq': 8.0,
     'L0_conv_wk': 3.997,
     'L0_conv_bk': 8.0,
     'L0_conv_b1': 2.85}
    for name, (base, spread) in spreads.items():
        noise = np.random.default_rng([zlib.crc32(name.encode()), seed]).standard_normal(out[name].shape)
        drawn = base * np.exp(spread * noise) if base else spread * noise
        out[name] = jnp.asarray(drawn.astype(out[name].dtype))
    for name, factor in factors.items():
        out[name] = (out[name] * factor).astype(out[name].dtype)
    return out
```

```python
import concourse.bass as bass
from concourse import mybir
from contextlib import ExitStack

F32 = mybir.dt.float32
BF16 = mybir.dt.bfloat16
ALU = mybir.AluOpType
ACT = mybir.ActivationFunctionType
AX = mybir.AxisListType

P = 128
H, D = 8, 16
SEQS = 4
T = SEQS * P
FF = 512
FC = FF // P
HU = 4
UNITS = SEQS * H // HU
VW = 32
EPS = 1e-5
HI, MID, LO = range(3)
Q_PARTS = (HI, HI, HI, MID, MID, LO)
K_PARTS = (HI, MID, LO, HI, MID, HI)
PROD = len(Q_PARTS) * D
MAXROWS = 3
UNROLL = 4
DMA = 16


def build(nc, x, wq, bq, wk, bk, wv, bv, wo, bo, w1, b1, w2, b2, g1, be1, g2, be2, out):
    n_seq = x.shape[0] * x.shape[1]
    G = n_seq // SEQS
    assert G % UNROLL == 0 and G >= 4 * UNROLL
    x_g = x.rearrange("b r k m -> (b r) k m").rearrange("(g s) k m -> g k s m", s=SEQS)
    out_g = out.rearrange("b r k m -> (b r) k m").rearrange("(g s) k m -> g k s m", s=SEQS)
    part_scr = nc.dram_tensor("part_scratch", [2, 6, D, H * T], BF16, kind="Internal").ap()
    max_scr = nc.dram_tensor("max_scratch", [MAXROWS, H * SEQS, P], BF16, kind="Internal").ap()

    with ExitStack() as ctx:
        def sb(name, shape, dt=F32):
            return ctx.enter_context(nc.sbuf_tensor(name, shape, dt))

        def sem(name):
            return ctx.enter_context(nc.semaphore(name))

        wq_in, wk_in = sb("wq_in", [P, H, D]), sb("wk_in", [P, H, D])
        wq_sb, wk_sb, wv_sb, wo_sb = (sb(n, [P, P]) for n in ("wq_sb", "wk_sb", "wv_sb", "wo_sb"))
        w1_sb, w2_sb = sb("w1_sb", [P, FF]), sb("w2_sb", [P, FC, P])
        bq_col, bk_col, bv_col, g1_col, be1_col = (sb(n, [P, 1]) for n in ("bq_col", "bk_col", "bv_col", "g1_col", "be1_col"))
        b1_col = sb("b1_col", [P, FC])
        bo_row, b2_row = sb("bo_row", [P, SEQS, P]), sb("b2_row", [P, SEQS, P])
        be1_row, g1_row = sb("be1_row", [P, SEQS, P]), sb("g1_row", [P, SEQS, P])
        g2_row, be2_row = sb("g2_row", [P, SEQS, P]), sb("be2_row", [P, SEQS, P])
        bv_wide, ident = sb("bv_wide", [P, P]), sb("ident", [P, P])
        minus_half, eps_sb, pause = sb("minus_half", [P, SEQS]), sb("eps_sb", [P, SEQS]), sb("pause", [P, 1])
        x_sb = sb("x_sb", [P, 2, SEQS, P])
        xb_sb = sb("xb_sb", [P, 4, SEQS, P])
        xT_sb = sb("xT_sb", [P, T])
        parts = sb("parts", [P, 2, 6, T], BF16)
        rest_sb = sb("rest_sb", [P, 2, T])
        stack = sb("stack", [PROD + MAXROWS, 4, 2, H, T], BF16)
        v_ones = sb("v_ones", [P, 4, SEQS, H, VW])
        max_sb = sb("max_sb", [P, 2, H, SEQS])
        max_parts = sb("max_parts", [H * SEQS, MAXROWS, P], BF16)
        max_rest = sb("max_rest", [H * SEQS, P])
        prob_sb = sb("prob_sb", [P, 4, HU * P])
        oT_sb = sb("oT_sb", [P, 2, HU * P])
        recip = sb("recip", [P, 4, HU])
        o_sb = sb("o_sb", [P, SEQS, P])
        onT_sb = sb("onT_sb", [P, T])
        z_sb, n_sb, x1_sb = sb("z_sb", [P, SEQS, P]), sb("n_sb", [P, SEQS, P]), sb("x1_sb", [P, SEQS, P])
        x1g_sb = sb("x1g_sb", [P, SEQS, P])
        x1T_sb = sb("x1T_sb", [P, T])
        h_sb = sb("h_sb", [P, FC, T])
        y_sb, m_sb, mg_sb = sb("y_sb", [P, SEQS, P]), sb("m_sb", [P, SEQS, P]), sb("mg_sb", [P, SEQS, P])
        out_sb = sb("out_sb", [P, 2, SEQS, P])
        st1, mv1, ve1, rs1 = sb("st1", [P, SEQS, 6]), sb("mv1", [P, SEQS, 2]), sb("ve1", [P, SEQS]), sb("rs1", [P, SEQS])
        st2, mv2, ve2, rs2 = sb("st2", [P, SEQS, 6]), sb("mv2", [P, SEQS, 2]), sb("ve2", [P, SEQS]), sb("rs2", [P, SEQS])
        s_ps = [ctx.enter_context(nc.psum_tensor(f"s_ps{b}", [P, T], F32)) for b in range(2)]
        sT_ps = [ctx.enter_context(nc.psum_tensor(f"sT_ps{b}", [P, T], F32)) for b in range(2)]
        oT_ps, A, B, C = (ctx.enter_context(nc.psum_tensor(n, [P, T], F32)) for n in ("oT_ps", "bankA", "bankB", "bankC"))

        consts_loaded, ident_zero, consts_set = sem("consts_loaded"), sem("ident_zero"), sem("consts_set")
        bv_wide_set, bv_wo_done, rows_set = sem("bv_wide_set"), sem("bv_wo_done"), sem("rows_set")
        x_loaded = [sem("x_loaded0"), sem("x_loaded1")]
        parts_written = [sem("parts_written0"), sem("parts_written1")]
        stack_loaded = [sem("stack_loaded0"), sem("stack_loaded1")]
        max_written, max_rows_loaded = sem("max_written"), sem("max_rows_loaded")
        out_stored = [sem("out_stored0"), sem("out_stored1")]
        xT_done, q_done, k_done, v_done = sem("xT_done"), sem("q_done"), sem("k_done"), sem("v_done")
        s_done, maxT_done, sT_done, pv_done = sem("s_done"), sem("maxT_done"), sem("sT_done"), sem("pv_done")
        o_back_done, onT_done, wo_done = sem("o_back_done"), sem("onT_done"), sem("wo_done")
        x1T_done, f1_done, f2_done = sem("x1T_done"), sem("f1_done"), sem("f2_done")
        xT_copied, hi_split, v_copied, exp_done = sem("xT_copied"), sem("hi_split"), sem("v_copied"), sem("exp_done")
        oT_copied, onT_copied, x1T_copied, h_ready = sem("oT_copied"), sem("onT_copied"), sem("x1T_copied"), sem("h_ready")
        rest_made, mid_split, max_done = sem("rest_made"), sem("mid_split"), sem("max_done")
        max_hi, max_rest_made, max_mid, max_parts_made = sem("max_hi"), sem("max_rest_made"), sem("max_mid"), sem("max_parts_made")
        recip_made, o_normed = sem("recip_made"), sem("o_normed")
        z_done, st1_done, mv1_done, n_done = sem("z_done"), sem("st1_done"), sem("mv1_done"), sem("n_done")
        y_done, st2_done, mv2_done, m_done = sem("y_done"), sem("st2_done"), sem("mv2_done"), sem("m_done")
        xb_done, lo_split, ve1_done, rs1_done = sem("xb_done"), sem("lo_split"), sem("ve1_done"), sem("rs1_done")
        x1g_done, x1_done, ve2_done, rs2_done = sem("x1g_done"), sem("x1_done"), sem("ve2_done"), sem("rs2_done")
        mg_done, out_ready = sem("mg_done"), sem("out_ready")

        def live(t, r, lag):
            return not isinstance(t, int) or 0 <= r - lag < G

        def upto(t, r, lag, per=1, plus=0):
            plus += per * (r - lag)
            if isinstance(t, int):
                return min(plus, per * G) if plus > 0 else None
            return t * per + plus if plus else t * per

        def upto_dma(t, r, lag, before=0, per=DMA):
            plus = per * ((r - lag) // 2 + 1 - before)
            if isinstance(t, int):
                return plus if plus > 0 else None
            return t * (per // 2) + plus if plus else t * (per // 2)

        def sT_unit(u):
            return (3, u + 5) if u < 3 else (2, u - 3)

        def pv_unit(u):
            return (3, u + 4) if u < 4 else (2, u - 4)

        def iterate(eng, step, first, last, lags):
            for r in range(first):
                step(0, r)
            with eng.Fori(first, last, UNROLL) as t:
                for r in range(UNROLL):
                    step(t, r)
            for r in range(last, G + lags):
                step(0, r)

        N_CONST = 18
        block = ctx.enter_context(nc.Block())

        @block.sync
        def _(sp):
            def row(v):
                return v.rearrange("(a b m) -> a b m", a=1, b=1).broadcast_to([P, SEQS, P])

            def col(v):
                return v.rearrange("(p a) -> p a", a=1)

            def by_feature(v):
                return v.rearrange("(h d a) -> d h a", h=H, a=1)

            sp.dma_start(x_sb[:, 0], x_g[0]).then_inc(x_loaded[0], DMA)
            for dst, src in ((wq_in[:].rearrange("p h d -> p (h d)"), wq), (wk_in[:].rearrange("p h d -> p (h d)"), wk), (wv_sb[:], wv), (wo_sb[:], wo), (w1_sb[:], w1),
                             (w2_sb[:], w2.rearrange("(c p) m -> p c m", p=P)),
                             (bq_col[:], by_feature(bq)), (bk_col[:], by_feature(bk)), (bv_col[:], col(bv)),
                             (g1_col[:], col(g1)), (be1_col[:], col(be1)),
                             (b1_col[:], b1.rearrange("(c p) -> p c", p=P)),
                             (bo_row[:], row(bo)), (b2_row[:], row(b2)), (be1_row[:], row(be1)),
                             (g1_row[:], row(g1)), (g2_row[:], row(g2)), (be2_row[:], row(be2))):
                sp.dma_start(dst, src, allow_slow_non_contiguous=True).then_inc(consts_loaded, DMA)

            def step(t, r):
                if live(t, r, -1):
                    if (v := upto(t, r, 0)) is not None:
                        sp.wait_ge(xT_done, v)
                    if (v := upto(t, r, 0)) is not None:
                        sp.wait_ge(xb_done, v)
                    sp.dma_start(x_sb[:, (r + 1) % 2], x_g[t + (r + 1)]).then_inc(x_loaded[(r + 1) % 2], DMA)
                if live(t, r, 2):
                    sp.wait_ge(max_parts_made, upto(t, r, 2, plus=1))
                    sp.dma_start(max_scr.rearrange("a b k -> b a k"), max_parts[:]).then_inc(max_written, DMA)
                    sp.wait_ge(max_written, upto(t, r, 2, per=DMA, plus=DMA))
                    sp.dma_start(stack[PROD:PROD + MAXROWS, (r - 2) % 4, 0].rearrange("p h x -> p (h x)"),
                                 max_scr.rearrange("a b k -> a (b k)")).then_inc(max_rows_loaded, DMA)
                if live(t, r, 5):
                    sp.wait_ge(out_ready, upto(t, r, 5, plus=1))
                    sp.dma_start(out_g[t + (r - 5)], out_sb[:, (r - 5) % 2]).then_inc(out_stored[(r - 5) % 2], DMA)
                if live(t, r, 0):
                    sp.wait_ge(lo_split, upto(t, r, 0, per=2, plus=2))
                    scr = part_scr[r % 2]
                    sp.dma_start(scr.rearrange("c d (h x) -> (d h) c x", h=H), parts[:, r % 2]).then_inc(parts_written[r % 2], DMA)
                    sp.wait_ge(parts_written[r % 2], upto_dma(t, r, 0))
                    for j in range(6):
                        a, b = Q_PARTS[j], 3 + K_PARTS[j]
                        sp.dma_start(stack[j * D:(j + 1) * D, r % 4].rearrange("d c h x -> d c (h x)"),
                                     scr[a:b + 1:b - a].rearrange("c d x -> d c x")).then_inc(stack_loaded[r % 2], DMA)

            iterate(sp, step, 2 * UNROLL, G - UNROLL, 5)
            sp.wait_ge(out_stored[(G - 2) % 2], upto_dma(0, G - 2, 0))
            sp.wait_ge(out_stored[(G - 1) % 2], upto_dma(0, G - 1, 0))

        @block.gpsimd
        def _(pool):
            pool.memset(ident[:], 0.0).then_inc(ident_zero, 1)
            pool.memset(v_ones[:], 1.0).then_inc(consts_set, 1)
            pool.memset(minus_half[:], -0.5).then_inc(consts_set, 1)
            pool.memset(eps_sb[:], EPS).then_inc(consts_set, 1)
            pool.wait_ge(ident_zero, 1)
            pool.affine_select(out=ident[:], in_=ident[:], compare_op=ALU.not_equal, fill=1.0, base=0,
                               pattern=[[-1, P]], channel_multiplier=1).then_inc(consts_set, 1)
            pool.wait_ge(rows_set, 4)

            def lo_part(t, r, c):
                pool.wait_ge(mid_split, upto(t, r, 0, per=2, plus=c + 1))
                if (v := upto_dma(t, r, 0, before=1)) is not None:
                    pool.wait_ge(parts_written[r % 2], v)
                pool.tensor_tensor(parts[:, r % 2, 3 * c + LO], rest_sb[:, c], parts[:, r % 2, 3 * c + MID],
                                   ALU.subtract).then_inc(lo_split, 1)

            def step(t, r):
                if live(t, r, 5):
                    pool.wait_ge(mv2_done, upto(t, r, 5, plus=1))
                    if (v := upto(t, r, 5)) is not None:
                        pool.wait_ge(m_done, v)
                    pool.tensor_tensor(ve2[:], mv2[:, :, 1], eps_sb[:], ALU.add).then_inc(ve2_done, 1)
                    pool.wait_ge(ve2_done, upto(t, r, 5, plus=1))
                    pool.tensor_tensor(rs2[:], ve2[:], minus_half[:], ALU.pow).then_inc(rs2_done, 1)
                if live(t, r, 0):
                    pool.wait_ge(x_loaded[r % 2], upto_dma(t, r, 0))
                    if (v := upto(t, r, 3)) is not None:
                        pool.wait_ge(z_done, v)
                    pool.tensor_tensor(xb_sb[:, r % 4], x_sb[:, r % 2], bo_row[:], ALU.add).then_inc(xb_done, 1)
                    lo_part(t, r, 0)
                if live(t, r, 5):
                    pool.wait_ge(m_done, upto(t, r, 5, plus=1))
                    if (v := upto(t, r, 5)) is not None:
                        pool.wait_ge(out_ready, v)
                    pool.tensor_tensor(mg_sb[:], m_sb[:], g2_row[:], ALU.mult).then_inc(mg_done, 1)
                    pool.wait_ge(mg_done, upto(t, r, 5, plus=1))
                    if (v := upto_dma(t, r, 5, before=1)) is not None:
                        pool.wait_ge(out_stored[(r - 5) % 2], v)
                    pool.tensor_tensor(out_sb[:, (r - 5) % 2], mg_sb[:], be2_row[:], ALU.add).then_inc(out_ready, 1)
                if live(t, r, 0):
                    lo_part(t, r, 1)
                if live(t, r, 4):
                    pool.wait_ge(n_done, upto(t, r, 4, plus=1))
                    if (v := upto(t, r, 4)) is not None:
                        pool.wait_ge(x1_done, v)
                    pool.tensor_tensor(x1g_sb[:], n_sb[:], g1_row[:], ALU.mult).then_inc(x1g_done, 1)
                    pool.wait_ge(x1g_done, upto(t, r, 4, plus=1))
                    if (v := upto(t, r, 4, per=2)) is not None:
                        pool.wait_ge(y_done, v)
                    pool.tensor_tensor(x1_sb[:], x1g_sb[:], be1_row[:], ALU.add).then_inc(x1_done, 1)
                if live(t, r, 3):
                    pool.wait_ge(mv1_done, upto(t, r, 3, plus=1))
                    if (v := upto(t, r, 3)) is not None:
                        pool.wait_ge(n_done, v)
                    pool.tensor_tensor(ve1[:], mv1[:, :, 1], eps_sb[:], ALU.add).then_inc(ve1_done, 1)
                    pool.wait_ge(ve1_done, upto(t, r, 3, plus=1))
                    pool.tensor_tensor(rs1[:], ve1[:], minus_half[:], ALU.pow).then_inc(rs1_done, 1)

            iterate(pool, step, 2 * UNROLL, G, 5)

        @block.scalar
        def _(act):
            act.wait_ge(consts_loaded, N_CONST * DMA)
            act.wait_ge(consts_set, 5)

            def hi_part(t, r, c):
                act.wait_ge((q_done, k_done)[c], upto(t, r, 0, plus=1))
                if (v := upto_dma(t, r, 0, before=1)) is not None:
                    act.wait_ge(parts_written[r % 2], v)
                act.activation(parts[:, r % 2, 3 * c + HI], (B, A)[c][:], ACT.Identity,
                               bias=(bq_col, bk_col)[c][:]).then_inc(hi_split, 1)

            def relu(t, r, c):
                act.wait_ge(f1_done, upto(t, r, 4, per=FC, plus=c + 1))
                if (v := upto(t, r, 4, per=2)) is not None:
                    act.wait_ge(f2_done, v)
                act.activation(h_sb[:, c], (B, C)[c % 2][:], ACT.Relu, bias=b1_col[:, c:c + 1]).then_inc(h_ready, 1)

            def copy_oT(t, r, lag, half):
                act.wait_ge(pv_done, upto(t, r, lag, per=UNITS, plus=4 * half + 4))
                if (v := upto(t, r, lag, per=2, plus=half - 1)) is not None:
                    act.wait_ge(o_back_done, v)
                act.activation(oT_sb[:, half], oT_ps[:], ACT.Copy).then_inc(oT_copied, 1)

            def copy_onT(t, r, half):
                act.wait_ge(onT_done, upto(t, r, 3, per=2, plus=half + 1))
                if (v := upto(t, r, 3)) is not None:
                    act.wait_ge(wo_done, v)
                cols = slice(half * 2 * P, (half + 1) * 2 * P)
                act.activation(onT_sb[:, cols], A[:, cols], ACT.Copy).then_inc(onT_copied, 1)

            def step(t, r):
                for u in range(UNITS):
                    lag, unit = sT_unit(u)
                    if live(t, r, lag):
                        n = (UNITS * (r - lag) + unit)
                        act.wait_ge(sT_done, upto(t, r, lag, per=UNITS, plus=unit + 1))
                        if (v := upto(t, r, lag, per=UNITS, plus=unit - 3)) is not None:
                            act.wait_ge(pv_done, v)
                        act.activation(prob_sb[:, n % 4], sT_ps[n % 2][:], ACT.Exp,
                                       scale=float(D) ** -0.5).then_inc(exp_done, 1)
                    if u == 0 and live(t, r, 0):
                        act.wait_ge(xT_done, upto(t, r, 0, plus=1))
                        if (v := upto(t, r, 0)) is not None:
                            act.wait_ge(v_done, v)
                        act.activation(xT_sb[:], C[:], ACT.Copy).then_inc(xT_copied, 1)
                    if u == 1 and live(t, r, 3):
                        copy_onT(t, r, 0)
                    if u == 1 and live(t, r, 4):
                        act.wait_ge(x1T_done, upto(t, r, 4, plus=1))
                        if (v := upto(t, r, 4, per=FC)) is not None:
                            act.wait_ge(f1_done, v)
                        act.activation(x1T_sb[:], C[:], ACT.Identity, bias=be1_col[:],
                                       scale=g1_col[:]).then_inc(x1T_copied, 1)
                    if u == 1 and live(t, r, 0):
                        hi_part(t, r, 0)
                    if u == 2 and live(t, r, 0):
                        hi_part(t, r, 1)
                    if u == 3 and live(t, r, 3):
                        copy_oT(t, r, 3, 1)
                    if u == 3 and live(t, r, 0):
                        act.wait_ge(v_done, upto(t, r, 0, plus=1))
                        if (v := upto(t, r, 3, per=UNITS)) is not None:
                            act.wait_ge(pv_done, v)
                        act.activation(v_ones[:, r % 4, :, :, 0:D],
                                       A[:].rearrange("p (s h d) -> p s h d", s=SEQS, h=H),
                                       ACT.Copy).then_inc(v_copied, 1)
                    if u in (2, 3, 4, 5) and live(t, r, 4):
                        relu(t, r, u - 2)
                    if u == 5 and live(t, r, 3):
                        copy_onT(t, r, 1)
                    if u == 7 and live(t, r, 2):
                        copy_oT(t, r, 2, 0)

            iterate(act, step, 2 * UNROLL, G, 4)

        @block.vector
        def _(dve):
            dve.memset(stack[PROD:PROD + MAXROWS, :, 1], 1.0).then_inc(consts_set, 1)
            dve.wait_ge(consts_loaded, N_CONST * DMA)
            dve.wait_ge(consts_set, 5)
            for w_sb, w_in in ((wq_sb, wq_in), (wk_sb, wk_in)):
                dve.tensor_copy(w_sb[:].rearrange("p (d h) -> p h d", h=H), w_in[:]).then_inc(rows_set, 1)
            dve.tensor_scalar(bv_wide[:], ident[:], 0.0, bv_col[:], ALU.mult, ALU.add).then_inc(bv_wide_set, 1)
            dve.tensor_tensor(be1_row[:], be1_row[:], b2_row[:], ALU.add).then_inc(rows_set, 1)
            dve.wait_ge(bv_wo_done, 1)
            dve.tensor_tensor(bo_row[:], A[:].rearrange("p (s m) -> p s m", s=SEQS), bo_row[:],
                              ALU.add).then_inc(rows_set, 1)

            def split(t, r, c):
                dve.wait_ge(hi_split, upto(t, r, 0, per=2, plus=c + 1))
                if (v := upto(t, r, 0, per=2, plus=c - 1)) is not None:
                    dve.wait_ge(lo_split, v)
                dve.scalar_tensor_tensor(rest_sb[:, c], (B, A)[c][:], (bq_col, bk_col)[c][:],
                                         parts[:, r % 2, 3 * c + HI], ALU.add, ALU.subtract).then_inc(rest_made, 1)
                dve.wait_ge(rest_made, upto(t, r, 0, per=2, plus=c + 1))
                if (v := upto_dma(t, r, 0, before=1)) is not None:
                    dve.wait_ge(parts_written[r % 2], v)
                dve.tensor_copy(parts[:, r % 2, 3 * c + MID], rest_sb[:, c]).then_inc(mid_split, 1)

            def normalise(t, r, half):
                o = A[:].rearrange("p (c w) -> p c w", w=VW)
                k = 2 * half
                dve.wait_ge(o_back_done, upto(t, r, 3, per=2, plus=half + 1))
                if (v := upto(t, r, 3, per=2, plus=half)) is not None:
                    dve.wait_ge(o_normed, v)
                dve.reciprocal(recip[:].rearrange("p c h -> p (c h)"), o[:, :, D]).then_inc(recip_made, 1)
                dve.wait_ge(recip_made, upto(t, r, 3, per=2, plus=half + 1))
                if (v := upto(t, r, 3, per=2, plus=half - 1)) is not None:
                    dve.wait_ge(onT_done, v)
                dve.tensor_tensor(o_sb[:, k:k + 2].rearrange("p s (h d) -> p (s h) d", d=D), o[:, :, 0:D],
                                  recip[:].rearrange("p c h -> p (c h)").unsqueeze(2).broadcast_to([P, 16, D]),
                                  ALU.mult).then_inc(o_normed, 1)

            def add_y(t, r, lag, half):
                k = 2 * half
                dve.wait_ge(f2_done, upto(t, r, lag, per=2, plus=half + 1))
                dve.wait_ge(x1_done, upto(t, r, lag, plus=1))
                if (v := upto(t, r, lag)) is not None:
                    dve.wait_ge(m_done, v)
                if (v := upto(t, r, lag)) is not None:
                    dve.wait_ge(mv2_done, v)
                dve.tensor_tensor(y_sb[:, k:k + 2], (B, C)[half][:, 0:2 * P].rearrange("p (s m) -> p s m", s=2),
                                  x1_sb[:, k:k + 2], ALU.add).then_inc(y_done, 1)

            def statistics(t, r, lag, src, st, mv, st_done, mv_done, mv_used):
                for s in range(SEQS):
                    ins = dve.bn_stats(st[:, s], src[:, s])
                ins.then_inc(st_done, 1)
                dve.wait_ge(st_done, upto(t, r, lag, plus=1))
                if (v := upto(t, r, lag)) is not None:
                    dve.wait_ge(mv_used, v)
                dve.memset(pause[:], 0.0)
                for s in range(SEQS):
                    ins = dve.bn_aggr(mv[:, s], st[:, s])
                ins.then_inc(mv_done, 1)

            def step(t, r):
                for u in range(UNITS):
                    if u == 0 and live(t, r, 5):
                        add_y(t, r, 5, 1)
                    if live(t, r, 1):
                        n = UNITS * (r - 1) + u
                        s, half = u // 2, u % 2
                        dve.wait_ge(s_done, upto(t, r, 1, per=UNITS, plus=u + 1))
                        if (v := upto(t, r, 2)) is not None:
                            dve.wait_ge(maxT_done, v)
                        dve.reduce_max(max_sb[:, (r - 1) % 2, half * HU:(half + 1) * HU, s],
                                       s_ps[n % 2][:].rearrange("p (h k) -> p h k", h=HU), AX.X).then_inc(max_done, 1)
                    if u == 0 and live(t, r, 2):
                        mT = B[0:H * SEQS, 0:P]
                        dve.wait_ge(maxT_done, upto(t, r, 2, plus=1))
                        if (v := upto(t, r, 2, per=DMA)) is not None:
                            dve.wait_ge(max_written, v)
                        dve.tensor_scalar(max_parts[:, HI], mT, -1.0, None, ALU.mult).then_inc(max_hi, 1)
                        dve.wait_ge(max_hi, upto(t, r, 2, plus=1))
                        dve.scalar_tensor_tensor(max_rest[:], mT, -1.0, max_parts[:, HI],
                                                 ALU.mult, ALU.subtract).then_inc(max_rest_made, 1)
                        dve.wait_ge(max_rest_made, upto(t, r, 2, plus=1))
                        dve.tensor_copy(max_parts[:, MID], max_rest[:]).then_inc(max_mid, 1)
                        dve.wait_ge(max_mid, upto(t, r, 2, plus=1))
                        dve.tensor_tensor(max_parts[:, LO], max_rest[:], max_parts[:, MID],
                                          ALU.subtract).then_inc(max_parts_made, 1)
                    if u == 0 and live(t, r, 3):
                        normalise(t, r, 0)
                    if u == 0 and live(t, r, 5):
                        dve.wait_ge(y_done, upto(t, r, 5, per=2, plus=2))
                        statistics(t, r, 5, y_sb, st2, mv2, st2_done, mv2_done, m_done)
                    if u == 1 and live(t, r, 0):
                        split(t, r, 0)
                    if u == 1 and live(t, r, 5):
                        dve.wait_ge(rs2_done, upto(t, r, 5, plus=1))
                        if (v := upto(t, r, 5)) is not None:
                            dve.wait_ge(mg_done, v)
                        for s in range(SEQS):
                            ins = dve.tensor_scalar(m_sb[:, s], y_sb[:, s], mv2[:, s, 0:1], rs2[:, s:s + 1],
                                                    ALU.subtract, ALU.mult)
                        ins.then_inc(m_done, 1)
                    if u == 2 and live(t, r, 0):
                        split(t, r, 1)
                    if u == 4 and live(t, r, 3):
                        normalise(t, r, 1)
                    if u == 6 and live(t, r, 3):
                        dve.wait_ge(wo_done, upto(t, r, 3, plus=1))
                        dve.wait_ge(xb_done, upto(t, r, 3, plus=1))
                        if (v := upto(t, r, 3)) is not None:
                            dve.wait_ge(n_done, v)
                        if (v := upto(t, r, 3)) is not None:
                            dve.wait_ge(mv1_done, v)
                        dve.tensor_tensor(z_sb[:], A[:].rearrange("p (s m) -> p s m", s=SEQS), xb_sb[:, (r - 3) % 4],
                                          ALU.add).then_inc(z_done, 1)
                        dve.wait_ge(z_done, upto(t, r, 3, plus=1))
                        statistics(t, r, 3, z_sb, st1, mv1, st1_done, mv1_done, n_done)
                    if u == 7 and live(t, r, 4):
                        add_y(t, r, 4, 0)
                    if u == 7 and live(t, r, 3):
                        dve.wait_ge(rs1_done, upto(t, r, 3, plus=1))
                        if (v := upto(t, r, 3)) is not None:
                            dve.wait_ge(x1T_done, v)
                        if (v := upto(t, r, 3)) is not None:
                            dve.wait_ge(x1g_done, v)
                        for s in range(SEQS):
                            ins = dve.tensor_scalar(n_sb[:, s], z_sb[:, s], mv1[:, s, 0:1], rs1[:, s:s + 1],
                                                    ALU.subtract, ALU.mult)
                        ins.then_inc(n_done, 1)

            iterate(dve, step, 2 * UNROLL, G, 5)

        @block.tensor
        def _(pe):
            pe.wait_ge(consts_loaded, N_CONST * DMA)
            pe.wait_ge(consts_set, 5)
            pe.wait_ge(bv_wide_set, 1)
            for s in range(SEQS):
                ins = pe.matmul(A[:, s * P:(s + 1) * P], bv_wide[:], wo_sb[:], start=True, stop=True)
            ins.then_inc(bv_wo_done, 1)
            pe.wait_ge(rows_set, 4)

            def transposes(bank, srcs):
                for k, src in enumerate(srcs):
                    ins = pe.transpose(bank[:, k * P:(k + 1) * P], src, ident[:])
                return ins

            def hidden(t, r, c):
                if c == 0:
                    pe.wait_ge(x1T_copied, upto(t, r, 4, plus=1))
                    pe.wait_ge(rest_made, upto(t, r, 0, per=2, plus=1))
                    if not live(t, r, 0):
                        pe.wait_ge(max_rest_made, upto(t, r, 2, plus=1))
                        pe.wait_ge(y_done, upto(t, r, 5, per=2, plus=1))
                elif c == 1:
                    pe.wait_ge(x1T_copied, upto(t, r, 4, plus=1))
                else:
                    pe.wait_ge(h_ready, upto(t, r, 4, per=FC, plus=c - 1))
                pe.matmul((B, C)[c % 2][:], w1_sb[:, c * P:(c + 1) * P], x1T_sb[:], start=True,
                          stop=True).then_inc(f1_done, 1)

            def down(t, r, half):
                pe.wait_ge(h_ready, upto(t, r, 4, per=FC, plus=FC))
                for s in range(2):
                    tok = slice((2 * half + s) * P, (2 * half + s + 1) * P)
                    for c in range(FC):
                        ins = pe.matmul((B, C)[half][:, s * P:(s + 1) * P], h_sb[:, c, tok], w2_sb[:, c],
                                        start=c == 0, stop=c == FC - 1)
                ins.then_inc(f2_done, 1)

            def o_back(t, r, half):
                pe.wait_ge(oT_copied, upto(t, r, 3, per=2, plus=half + 1))
                transposes(A, [oT_sb[:, half, k * P:(k + 1) * P] for k in range(4)]).then_inc(o_back_done, 1)

            def onT(t, r, half):
                pe.wait_ge(o_normed, upto(t, r, 3, per=2, plus=half + 1))
                for s in (2 * half, 2 * half + 1):
                    ins = pe.transpose(A[:, s * P:(s + 1) * P], o_sb[:, s], ident[:])
                ins.then_inc(onT_done, 1)

            def step(t, r):
                for u in range(UNITS):
                    if live(t, r, 1):
                        n, s = UNITS * (r - 1) + u, u // 2
                        tok = slice(s * P, (s + 1) * P)
                        if u == 0:
                            pe.wait_ge(stack_loaded[(r - 1) % 2], upto_dma(t, r, 1, per=6 * DMA))
                        if (v := upto(t, r, 1, per=UNITS, plus=u - 1)) is not None:
                            pe.wait_ge(max_done, v)
                        for j in range(HU):
                            h = HU * (u % 2) + j
                            ins = pe.matmul(s_ps[n % 2][:, j * P:(j + 1) * P], stack[0:PROD, (r - 1) % 4, 0, h, tok],
                                            stack[0:PROD, (r - 1) % 4, 1, h, tok], start=True, stop=True)
                        ins.then_inc(s_done, 1)
                    lag, unit = sT_unit(u)
                    if live(t, r, lag):
                        n, s = UNITS * (r - lag) + unit, unit // 2
                        tok = slice(s * P, (s + 1) * P)
                        if unit == 0:
                            pe.wait_ge(max_rows_loaded, upto(t, r, lag, per=DMA, plus=DMA))
                        if (v := upto(t, r, lag, per=UNITS, plus=unit - 1)) is not None:
                            pe.wait_ge(exp_done, v)
                        for j in range(HU):
                            h = HU * (unit % 2) + j
                            ins = pe.matmul(sT_ps[n % 2][:, j * P:(j + 1) * P], stack[:, (r - lag) % 4, 1, h, tok],
                                            stack[:, (r - lag) % 4, 0, h, tok], start=True, stop=True)
                        ins.then_inc(sT_done, 1)
                    if u == 0:
                        if live(t, r, 2):
                            pe.wait_ge(max_done, upto(t, r, 2, per=UNITS, plus=UNITS))
                            if (v := upto(t, r, 5, per=2, plus=1)) is not None:
                                pe.wait_ge(y_done, v)
                            pe.transpose(B[0:H * SEQS, 0:P], max_sb[:, r % 2].rearrange("p h s -> p (h s)"),
                                         ident[:]).then_inc(maxT_done, 1)
                        if live(t, r, 3):
                            if (v := upto(t, r, 4, plus=1)) is not None:
                                pe.wait_ge(z_done, v)
                            o_back(t, r, 0)
                        if live(t, r, 0):
                            pe.wait_ge(x_loaded[r % 2], upto_dma(t, r, 0))
                            if (v := upto(t, r, 5, per=2, plus=2)) is not None:
                                pe.wait_ge(y_done, v)
                            transposes(C, [x_sb[:, r % 2, s] for s in range(SEQS)]).then_inc(xT_done, 1)
                    if u == 1:
                        if live(t, r, 3):
                            onT(t, r, 0)
                        if live(t, r, 4):
                            pe.wait_ge(n_done, upto(t, r, 4, plus=1))
                            pe.wait_ge(xT_copied, upto(t, r, 0, plus=1))
                            if not live(t, r, 0):
                                pe.wait_ge(y_done, upto(t, r, 5, per=2, plus=2))
                            transposes(C, [n_sb[:, s] for s in range(SEQS)]).then_inc(x1T_done, 1)
                        if live(t, r, 0):
                            pe.wait_ge(xT_copied, upto(t, r, 0, plus=1))
                            if (v := upto(t, r, 2, plus=1)) is not None:
                                pe.wait_ge(max_rest_made, v)
                            pe.matmul(B[:], wq_sb[:], xT_sb[:], start=True, stop=True).then_inc(q_done, 1)
                    if u == 2:
                        if live(t, r, 0):
                            if (v := upto(t, r, 3, per=2, plus=1)) is not None:
                                pe.wait_ge(onT_copied, v)
                            pe.matmul(A[:], wk_sb[:], xT_sb[:], start=True, stop=True).then_inc(k_done, 1)
                        if live(t, r, 4):
                            hidden(t, r, 0)
                    if u == 3:
                        if live(t, r, 0):
                            pe.wait_ge(rest_made, upto(t, r, 0, per=2, plus=2))
                            for s in range(SEQS):
                                ins = pe.matmul(A[:, s * P:(s + 1) * P], xT_sb[:, s * P:(s + 1) * P], wv_sb[:],
                                                start=True, stop=True)
                            ins.then_inc(v_done, 1)
                        if live(t, r, 4):
                            hidden(t, r, 1)
                    if u == 4:
                        if live(t, r, 3):
                            pe.wait_ge(v_copied, upto(t, r, 0, plus=1))
                            if not live(t, r, 0):
                                pe.wait_ge(onT_copied, upto(t, r, 3, per=2, plus=1))
                            o_back(t, r, 1)
                        if live(t, r, 4):
                            hidden(t, r, 2)
                    if u == 5:
                        if live(t, r, 3):
                            onT(t, r, 1)
                        if live(t, r, 4):
                            hidden(t, r, 3)
                    if u == 6:
                        if live(t, r, 3):
                            pe.wait_ge(onT_copied, upto(t, r, 3, per=2, plus=2))
                            for s in range(SEQS):
                                ins = pe.matmul(A[:, s * P:(s + 1) * P], onT_sb[:, s * P:(s + 1) * P], wo_sb[:],
                                                start=True, stop=True)
                            ins.then_inc(wo_done, 1)
                        if live(t, r, 4):
                            down(t, r, 0)
                    if u == 7 and live(t, r, 4):
                        down(t, r, 1)
                    lag, unit = pv_unit(u)
                    if live(t, r, lag):
                        n, s = UNITS * (r - lag) + unit, unit // 2
                        pe.wait_ge(exp_done, upto(t, r, lag, per=UNITS, plus=unit + 1))
                        if unit == 0:
                            pe.wait_ge(v_copied, upto(t, r, lag, plus=1))
                        if unit % 4 == 0:
                            if (v := upto(t, r, lag, per=2, plus=unit // 4)) is not None:
                                pe.wait_ge(oT_copied, v)
                        for j in range(HU):
                            h = HU * (unit % 2) + j
                            ins = pe.matmul(oT_ps[j * VW:(j + 1) * VW, (unit % 4) * P:(unit % 4 + 1) * P],
                                            v_ones[:, (r - lag) % 4, s, h], prob_sb[:, n % 4, j * P:(j + 1) * P],
                                            start=True, stop=True)
                        ins.then_inc(pv_done, 1)

            iterate(pe, step, 2 * UNROLL, G, 4)


NAMES = ["wq", "bq", "wk", "bk", "wv", "bv", "wo", "bo", "w1", "b1", "w2", "b2", "ln1_g", "ln1_b", "ln2_g", "ln2_b"]


def kernel(**inputs):
    import numpy as _np
    import concourse.bacc as _bacc
    from concourse import mybir as _mybir
    from concourse.bass_utils import run_bass_kernel_spmd as _run

    nc = _bacc.Bacc("TRN2", target_bir_lowering=False, num_devices=1)
    arrays, args = {}, []
    for name in ["x"] + ["L0_conv_" + n for n in NAMES]:
        a = _np.ascontiguousarray(inputs[name])
        arrays[f"in_{name}"] = a
        args.append(nc.dram_tensor(f"in_{name}", a.shape, _mybir.dt.from_np(a.dtype), kind="ExternalInput").ap())
    out = nc.dram_tensor("out", arrays["in_x"].shape, F32, kind="ExternalOutput").ap()
    build(nc, *args, out)
    return _run(nc, [arrays], core_ids=[0]).results[0]["out"]
```

```python
import concourse.bass as bass
from concourse import mybir
from contextlib import ExitStack

F32 = mybir.dt.float32
BF16 = mybir.dt.bfloat16
ALU = mybir.AluOpType
ACT = mybir.ActivationFunctionType
AX = mybir.AxisListType

P = 128
H, D = 8, 16
SEQS = 4
T = SEQS * P
FF = 512
FC = FF // P
HU = 4
UNITS = SEQS * H // HU
VW = 32
EPS = 1e-5
HI, MID, LO = range(3)
Q_PARTS = (HI, HI, HI, MID, MID, LO)
K_PARTS = (HI, MID, LO, HI, MID, HI)
PROD = len(Q_PARTS) * D
MAXROWS = 3
UNROLL = 4
DMA = 16


def build(nc, x, wq, bq, wk, bk, wv, bv, wo, bo, w1, b1, w2, b2, g1, be1, g2, be2, out):
    n_seq = x.shape[0] * x.shape[1]
    G = n_seq // SEQS
    assert G % UNROLL == 0 and G >= 4 * UNROLL
    x_g = x.rearrange("b r k m -> (b r) k m").rearrange("(g s) k m -> g k s m", s=SEQS)
    out_g = out.rearrange("b r k m -> (b r) k m").rearrange("(g s) k m -> g k s m", s=SEQS)
    part_scr = nc.dram_tensor("part_scratch", [2, 6, D, H * T], BF16, kind="Internal").ap()
    max_scr = nc.dram_tensor("max_scratch", [MAXROWS, H * SEQS, P], BF16, kind="Internal").ap()

    with ExitStack() as ctx:
        def sb(name, shape, dt=F32):
            return ctx.enter_context(nc.sbuf_tensor(name, shape, dt))

        def sem(name):
            return ctx.enter_context(nc.semaphore(name))

        wq_in, wk_in = sb("wq_in", [P, H, D]), sb("wk_in", [P, H, D])
        wq_sb, wk_sb, wv_sb, wo_sb = (sb(n, [P, P]) for n in ("wq_sb", "wk_sb", "wv_sb", "wo_sb"))
        w1_sb, w2_sb = sb("w1_sb", [P, FF]), sb("w2_sb", [P, FC, P])
        bq_col, bk_col, bv_col, g1_col, be1_col = (sb(n, [P, 1]) for n in ("bq_col", "bk_col", "bv_col", "g1_col", "be1_col"))
        b1_col = sb("b1_col", [P, FC])
        bo_row, b2_row = sb("bo_row", [P, SEQS, P]), sb("b2_row", [P, SEQS, P])
        be1_row, g1_row = sb("be1_row", [P, SEQS, P]), sb("g1_row", [P, SEQS, P])
        g2_row, be2_row = sb("g2_row", [P, SEQS, P]), sb("be2_row", [P, SEQS, P])
        bv_wide, ident = sb("bv_wide", [P, P]), sb("ident", [P, P])
        minus_half, eps_sb, pause = sb("minus_half", [P, SEQS]), sb("eps_sb", [P, SEQS]), sb("pause", [P, 1])
        x_sb = sb("x_sb", [P, 2, SEQS, P])
        xb_sb = sb("xb_sb", [P, 4, SEQS, P])
        xT_sb = sb("xT_sb", [P, 2, T])
        parts = sb("parts", [P, 2, 6, T], BF16)
        rest_sb = sb("rest_sb", [P, 2, T])
        stack = sb("stack", [PROD + MAXROWS, 4, 2, H, T], BF16)
        v_ones = sb("v_ones", [P, 4, SEQS, H, VW])
        max_sb = sb("max_sb", [P, 2, H, SEQS])
        max_parts = sb("max_parts", [H * SEQS, MAXROWS, P], BF16)
        max_rest = sb("max_rest", [H * SEQS, P])
        prob_sb = sb("prob_sb", [P, 4, HU * P])
        oT_sb = sb("oT_sb", [P, 2, HU * P])
        recip = sb("recip", [P, 4, HU])
        o_sb = sb("o_sb", [P, SEQS, P])
        onT_sb = sb("onT_sb", [P, T])
        z_sb, n_sb, x1_sb = sb("z_sb", [P, SEQS, P]), sb("n_sb", [P, SEQS, P]), sb("x1_sb", [P, SEQS, P])
        x1g_sb = sb("x1g_sb", [P, SEQS, P])
        x1T_sb = sb("x1T_sb", [P, T])
        h_sb = sb("h_sb", [P, FC, T])
        y_sb, m_sb, mg_sb = sb("y_sb", [P, SEQS, P]), sb("m_sb", [P, SEQS, P]), sb("mg_sb", [P, SEQS, P])
        out_sb = sb("out_sb", [P, 2, SEQS, P])
        st1, mv1, ve1, rs1 = sb("st1", [P, SEQS, 6]), sb("mv1", [P, SEQS, 2]), sb("ve1", [P, SEQS]), sb("rs1", [P, SEQS])
        st2, mv2, ve2, rs2 = sb("st2", [P, SEQS, 6]), sb("mv2", [P, SEQS, 2]), sb("ve2", [P, SEQS]), sb("rs2", [P, SEQS])
        s_ps = [ctx.enter_context(nc.psum_tensor(f"s_ps{b}", [P, T], F32)) for b in range(2)]
        sT_ps = [ctx.enter_context(nc.psum_tensor(f"sT_ps{b}", [P, T], F32)) for b in range(2)]
        oT_ps, A, B, C = (ctx.enter_context(nc.psum_tensor(n, [P, T], F32)) for n in ("oT_ps", "bankA", "bankB", "bankC"))

        consts_loaded, ident_zero, consts_set = sem("consts_loaded"), sem("ident_zero"), sem("consts_set")
        bv_wide_set, bv_wo_done, rows_set = sem("bv_wide_set"), sem("bv_wo_done"), sem("rows_set")
        x_loaded = [sem("x_loaded0"), sem("x_loaded1")]
        parts_written = [sem("parts_written0"), sem("parts_written1")]
        stack_loaded = [sem("stack_loaded0"), sem("stack_loaded1")]
        max_written, max_rows_loaded = sem("max_written"), sem("max_rows_loaded")
        out_stored = [sem("out_stored0"), sem("out_stored1")]
        xT_done, q_done, k_done, v_done = sem("xT_done"), sem("q_done"), sem("k_done"), sem("v_done")
        s_done, maxT_done, sT_done, pv_done = sem("s_done"), sem("maxT_done"), sem("sT_done"), sem("pv_done")
        o_back_done, onT_done, wo_done = sem("o_back_done"), sem("onT_done"), sem("wo_done")
        x1T_done, f1_done, f2_done = sem("x1T_done"), sem("f1_done"), sem("f2_done")
        xT_copied, hi_split, v_copied, exp_done = sem("xT_copied"), sem("hi_split"), sem("v_copied"), sem("exp_done")
        oT_copied, onT_copied, x1T_copied, h_ready = sem("oT_copied"), sem("onT_copied"), sem("x1T_copied"), sem("h_ready")
        rest_made, mid_split, max_done = sem("rest_made"), sem("mid_split"), sem("max_done")
        max_hi, max_rest_made, max_mid, max_parts_made = sem("max_hi"), sem("max_rest_made"), sem("max_mid"), sem("max_parts_made")
        recip_made, o_normed = sem("recip_made"), sem("o_normed")
        z_done, st1_done, mv1_done, n_done = sem("z_done"), sem("st1_done"), sem("mv1_done"), sem("n_done")
        y_done, st2_done, mv2_done, m_done = sem("y_done"), sem("st2_done"), sem("mv2_done"), sem("m_done")
        xb_done, lo_split, ve1_done, rs1_done = sem("xb_done"), sem("lo_split"), sem("ve1_done"), sem("rs1_done")
        x1g_done, x1_done, ve2_done, rs2_done = sem("x1g_done"), sem("x1_done"), sem("ve2_done"), sem("rs2_done")
        mg_done, out_ready = sem("mg_done"), sem("out_ready")

        def live(t, r, lag):
            return not isinstance(t, int) or 0 <= r - lag < G

        def upto(t, r, lag, per=1, plus=0):
            plus += per * (r - lag)
            if isinstance(t, int):
                return min(plus, per * G) if plus > 0 else None
            return t * per + plus if plus else t * per

        def upto_dma(t, r, lag, before=0, per=DMA):
            plus = per * ((r - lag) // 2 + 1 - before)
            if isinstance(t, int):
                return plus if plus > 0 else None
            return t * (per // 2) + plus if plus else t * (per // 2)

        def sT_unit(u):
            return (4, u + 4) if u < 4 else (3, u - 4)

        def iterate(eng, step, first, last, lags):
            for r in range(first):
                step(0, r)
            with eng.Fori(first, last, UNROLL) as t:
                for r in range(UNROLL):
                    step(t, r)
            for r in range(last, G + lags):
                step(0, r)

        N_CONST = 18
        block = ctx.enter_context(nc.Block())

        @block.sync
        def _(sp):
            def row(v):
                return v.rearrange("(a b m) -> a b m", a=1, b=1).broadcast_to([P, SEQS, P])

            def col(v):
                return v.rearrange("(p a) -> p a", a=1)

            def by_feature(v):
                return v.rearrange("(h d a) -> d h a", h=H, a=1)

            sp.dma_start(x_sb[:, 0], x_g[0]).then_inc(x_loaded[0], DMA)
            for dst, src in ((wq_in[:].rearrange("p h d -> p (h d)"), wq), (wk_in[:].rearrange("p h d -> p (h d)"), wk), (wv_sb[:], wv), (wo_sb[:], wo), (w1_sb[:], w1),
                             (w2_sb[:], w2.rearrange("(c p) m -> p c m", p=P)),
                             (bq_col[:], by_feature(bq)), (bk_col[:], by_feature(bk)), (bv_col[:], col(bv)),
                             (g1_col[:], col(g1)), (be1_col[:], col(be1)),
                             (b1_col[:], b1.rearrange("(c p) -> p c", p=P)),
                             (bo_row[:], row(bo)), (b2_row[:], row(b2)), (be1_row[:], row(be1)),
                             (g1_row[:], row(g1)), (g2_row[:], row(g2)), (be2_row[:], row(be2))):
                sp.dma_start(dst, src, allow_slow_non_contiguous=True).then_inc(consts_loaded, DMA)

            def step(t, r):
                if live(t, r, -1):
                    if (v := upto(t, r, 0)) is not None:
                        sp.wait_ge(xT_done, v)
                    if (v := upto(t, r, 0)) is not None:
                        sp.wait_ge(xb_done, v)
                    sp.dma_start(x_sb[:, (r + 1) % 2], x_g[t + (r + 1)]).then_inc(x_loaded[(r + 1) % 2], DMA)
                if live(t, r, 3):
                    sp.wait_ge(max_parts_made, upto(t, r, 3, plus=1))
                    sp.dma_start(max_scr.rearrange("a b k -> b a k"), max_parts[:]).then_inc(max_written, DMA)
                    sp.wait_ge(max_written, upto(t, r, 3, per=DMA, plus=DMA))
                    sp.dma_start(stack[PROD:PROD + MAXROWS, (r - 3) % 4, 0].rearrange("p h x -> p (h x)"),
                                 max_scr.rearrange("a b k -> a (b k)")).then_inc(max_rows_loaded, DMA)
                if live(t, r, 7):
                    sp.wait_ge(out_ready, upto(t, r, 7, plus=1))
                    sp.dma_start(out_g[t + (r - 7)], out_sb[:, (r - 7) % 2]).then_inc(out_stored[(r - 7) % 2], DMA)
                if live(t, r, 0):
                    sp.wait_ge(lo_split, upto(t, r, 0, per=2, plus=2))
                    scr = part_scr[r % 2]
                    sp.dma_start(scr.rearrange("c d (h x) -> (d h) c x", h=H), parts[:, r % 2]).then_inc(parts_written[r % 2], DMA)
                    sp.wait_ge(parts_written[r % 2], upto_dma(t, r, 0))
                    for j in range(6):
                        a, b = Q_PARTS[j], 3 + K_PARTS[j]
                        sp.dma_start(stack[j * D:(j + 1) * D, r % 4].rearrange("d c h x -> d c (h x)"),
                                     scr[a:b + 1:b - a].rearrange("c d x -> d c x")).then_inc(stack_loaded[r % 2], DMA)

            iterate(sp, step, 2 * UNROLL, G - UNROLL, 7)
            sp.wait_ge(out_stored[(G - 2) % 2], upto_dma(0, G - 2, 0))
            sp.wait_ge(out_stored[(G - 1) % 2], upto_dma(0, G - 1, 0))

        @block.gpsimd
        def _(pool):
            pool.memset(ident[:], 0.0).then_inc(ident_zero, 1)
            pool.memset(v_ones[:], 1.0).then_inc(consts_set, 1)
            pool.memset(minus_half[:], -0.5).then_inc(consts_set, 1)
            pool.memset(eps_sb[:], EPS).then_inc(consts_set, 1)
            pool.wait_ge(ident_zero, 1)
            pool.affine_select(out=ident[:], in_=ident[:], compare_op=ALU.not_equal, fill=1.0, base=0,
                               pattern=[[-1, P]], channel_multiplier=1).then_inc(consts_set, 1)
            pool.wait_ge(rows_set, 4)

            def lo_part(t, r, c):
                pool.wait_ge(mid_split, upto(t, r, 0, per=2, plus=c + 1))
                if (v := upto_dma(t, r, 0, before=1)) is not None:
                    pool.wait_ge(parts_written[r % 2], v)
                pool.tensor_tensor(parts[:, r % 2, 3 * c + LO], rest_sb[:, c], parts[:, r % 2, 3 * c + MID],
                                   ALU.subtract).then_inc(lo_split, 1)

            def step(t, r):
                if live(t, r, 1):
                    pool.wait_ge(x_loaded[(r - 1) % 2], upto_dma(t, r, 1))
                    if (v := upto(t, r, 5, plus=1)) is not None:
                        pool.wait_ge(z_done, v)
                    pool.tensor_tensor(xb_sb[:, (r - 1) % 4], x_sb[:, (r - 1) % 2], bo_row[:],
                                       ALU.add).then_inc(xb_done, 1)
                if live(t, r, 5):
                    pool.wait_ge(n_done, upto(t, r, 5, plus=1))
                    if (v := upto(t, r, 5)) is not None:
                        pool.wait_ge(x1_done, v)
                    pool.tensor_tensor(x1g_sb[:], n_sb[:], g1_row[:], ALU.mult).then_inc(x1g_done, 1)
                    pool.wait_ge(x1g_done, upto(t, r, 5, plus=1))
                    if (v := upto(t, r, 5, per=2)) is not None:
                        pool.wait_ge(y_done, v)
                    pool.tensor_tensor(x1_sb[:], x1g_sb[:], be1_row[:], ALU.add).then_inc(x1_done, 1)
                if live(t, r, 0):
                    lo_part(t, r, 0)
                if live(t, r, 0):
                    lo_part(t, r, 1)
                if live(t, r, 6):
                    pool.wait_ge(mv2_done, upto(t, r, 6, plus=1))
                    if (v := upto(t, r, 6)) is not None:
                        pool.wait_ge(m_done, v)
                    pool.tensor_tensor(ve2[:], mv2[:, :, 1], eps_sb[:], ALU.add).then_inc(ve2_done, 1)
                    pool.wait_ge(ve2_done, upto(t, r, 6, plus=1))
                    pool.tensor_tensor(rs2[:], ve2[:], minus_half[:], ALU.pow).then_inc(rs2_done, 1)
                if live(t, r, 4):
                    pool.wait_ge(mv1_done, upto(t, r, 4, plus=1))
                    if (v := upto(t, r, 4)) is not None:
                        pool.wait_ge(n_done, v)
                    pool.tensor_tensor(ve1[:], mv1[:, :, 1], eps_sb[:], ALU.add).then_inc(ve1_done, 1)
                    pool.wait_ge(ve1_done, upto(t, r, 4, plus=1))
                    pool.tensor_tensor(rs1[:], ve1[:], minus_half[:], ALU.pow).then_inc(rs1_done, 1)
                if live(t, r, 6):
                    pool.wait_ge(m_done, upto(t, r, 6, plus=1))
                    if (v := upto(t, r, 6)) is not None:
                        pool.wait_ge(out_ready, v)
                    pool.tensor_tensor(mg_sb[:], m_sb[:], g2_row[:], ALU.mult).then_inc(mg_done, 1)
                    pool.wait_ge(mg_done, upto(t, r, 6, plus=1))
                    if (v := upto_dma(t, r, 6, before=1)) is not None:
                        pool.wait_ge(out_stored[(r - 6) % 2], v)
                    pool.tensor_tensor(out_sb[:, (r - 6) % 2], mg_sb[:], be2_row[:], ALU.add).then_inc(out_ready, 1)

            iterate(pool, step, 2 * UNROLL, G, 6)

        @block.scalar
        def _(act):
            act.wait_ge(consts_loaded, N_CONST * DMA)
            act.wait_ge(consts_set, 5)

            def hi_part(t, r, c):
                act.wait_ge((q_done, k_done)[c], upto(t, r, 0, plus=1))
                if (v := upto_dma(t, r, 0, before=1)) is not None:
                    act.wait_ge(parts_written[r % 2], v)
                act.activation(parts[:, r % 2, 3 * c + HI], (B, A)[c][:], ACT.Identity,
                               bias=(bq_col, bk_col)[c][:]).then_inc(hi_split, 1)

            def relu(t, r, c):
                act.wait_ge(f1_done, upto(t, r, 5, per=FC, plus=c + 1))
                if (v := upto(t, r, 5, per=2)) is not None:
                    act.wait_ge(f2_done, v)
                act.activation(h_sb[:, c], (B, C)[c % 2][:], ACT.Relu, bias=b1_col[:, c:c + 1]).then_inc(h_ready, 1)

            def copy_oT(t, r, lag, half):
                act.wait_ge(pv_done, upto(t, r, lag, per=UNITS, plus=4 * half + 4))
                if (v := upto(t, r, lag, per=2, plus=half - 1)) is not None:
                    act.wait_ge(o_back_done, v)
                act.activation(oT_sb[:, half], oT_ps[:], ACT.Copy).then_inc(oT_copied, 1)

            def copy_onT(t, r):
                act.wait_ge(onT_done, upto(t, r, 4, plus=1))
                if (v := upto(t, r, 4)) is not None:
                    act.wait_ge(wo_done, v)
                act.activation(onT_sb[:], A[:], ACT.Copy).then_inc(onT_copied, 1)

            def step(t, r):
                for u in range(UNITS):
                    if u == 0 and live(t, r, 4):
                        copy_oT(t, r, 4, 0)
                    if u == 4 and live(t, r, 4):
                        copy_oT(t, r, 4, 1)
                    lag, unit = sT_unit(u)
                    if live(t, r, lag):
                        n = (UNITS * (r - lag) + unit)
                        act.wait_ge(sT_done, upto(t, r, lag, per=UNITS, plus=unit + 1))
                        if (v := upto(t, r, lag, per=UNITS, plus=unit - 3)) is not None:
                            act.wait_ge(pv_done, v)
                        act.activation(prob_sb[:, n % 4], sT_ps[n % 2][:], ACT.Exp,
                                       scale=float(D) ** -0.5).then_inc(exp_done, 1)
                    if u == 1 and live(t, r, 0):
                        act.wait_ge(xT_done, upto(t, r, 0, plus=1))
                        if (v := upto(t, r, 0)) is not None:
                            act.wait_ge(k_done, v)
                        act.activation(xT_sb[:, r % 2], C[:], ACT.Copy).then_inc(xT_copied, 1)
                    if u == 2 and live(t, r, 0):
                        hi_part(t, r, 0)
                    if u == 2 and live(t, r, 1):
                        act.wait_ge(v_done, upto(t, r, 1, plus=1))
                        if (v := upto(t, r, 4, per=UNITS)) is not None:
                            act.wait_ge(pv_done, v)
                        act.activation(v_ones[:, (r - 1) % 4, :, :, 0:D],
                                       A[:].rearrange("p (s h d) -> p s h d", s=SEQS, h=H),
                                       ACT.Copy).then_inc(v_copied, 1)
                    if u == 2 and live(t, r, 5):
                        act.wait_ge(x1T_done, upto(t, r, 5, plus=1))
                        if (v := upto(t, r, 5, per=FC)) is not None:
                            act.wait_ge(f1_done, v)
                        act.activation(x1T_sb[:], C[:], ACT.Identity, bias=be1_col[:],
                                       scale=g1_col[:]).then_inc(x1T_copied, 1)
                    if u == 3 and live(t, r, 0):
                        hi_part(t, r, 1)
                    if u in (3, 4, 5, 6) and live(t, r, 5):
                        relu(t, r, u - 3)
                    if u == 5 and live(t, r, 4):
                        copy_onT(t, r)

            iterate(act, step, 2 * UNROLL, G, 5)

        @block.vector
        def _(dve):
            dve.memset(stack[PROD:PROD + MAXROWS, :, 1], 1.0).then_inc(consts_set, 1)
            dve.wait_ge(consts_loaded, N_CONST * DMA)
            dve.wait_ge(consts_set, 5)
            for w_sb, w_in in ((wq_sb, wq_in), (wk_sb, wk_in)):
                dve.tensor_copy(w_sb[:].rearrange("p (d h) -> p h d", h=H), w_in[:]).then_inc(rows_set, 1)
            dve.tensor_scalar(bv_wide[:], ident[:], 0.0, bv_col[:], ALU.mult, ALU.add).then_inc(bv_wide_set, 1)
            dve.tensor_tensor(be1_row[:], be1_row[:], b2_row[:], ALU.add).then_inc(rows_set, 1)
            dve.wait_ge(bv_wo_done, 1)
            dve.tensor_tensor(bo_row[:], A[:].rearrange("p (s m) -> p s m", s=SEQS), bo_row[:],
                              ALU.add).then_inc(rows_set, 1)

            def split(t, r, c):
                dve.wait_ge(hi_split, upto(t, r, 0, per=2, plus=c + 1))
                if (v := upto(t, r, 0, per=2, plus=c - 1)) is not None:
                    dve.wait_ge(lo_split, v)
                dve.scalar_tensor_tensor(rest_sb[:, c], (B, A)[c][:], (bq_col, bk_col)[c][:],
                                         parts[:, r % 2, 3 * c + HI], ALU.add, ALU.subtract).then_inc(rest_made, 1)
                dve.wait_ge(rest_made, upto(t, r, 0, per=2, plus=c + 1))
                if (v := upto_dma(t, r, 0, before=1)) is not None:
                    dve.wait_ge(parts_written[r % 2], v)
                dve.tensor_copy(parts[:, r % 2, 3 * c + MID], rest_sb[:, c]).then_inc(mid_split, 1)

            def normalise(t, r, half):
                o = A[:].rearrange("p (c w) -> p c w", w=VW)
                k = 2 * half
                dve.wait_ge(o_back_done, upto(t, r, 4, per=2, plus=half + 1))
                if (v := upto(t, r, 4, per=2, plus=half)) is not None:
                    dve.wait_ge(o_normed, v)
                dve.reciprocal(recip[:].rearrange("p c h -> p (c h)"), o[:, :, D]).then_inc(recip_made, 1)
                dve.wait_ge(recip_made, upto(t, r, 4, per=2, plus=half + 1))
                if (v := upto(t, r, 4)) is not None:
                    dve.wait_ge(onT_done, v)
                dve.tensor_tensor(o_sb[:, k:k + 2].rearrange("p s (h d) -> p (s h) d", d=D), o[:, :, 0:D],
                                  recip[:].rearrange("p c h -> p (c h)").unsqueeze(2).broadcast_to([P, 16, D]),
                                  ALU.mult).then_inc(o_normed, 1)

            def add_y(t, r, half):
                k = 2 * half
                dve.wait_ge(f2_done, upto(t, r, 6, per=2, plus=half + 1))
                dve.wait_ge(x1_done, upto(t, r, 6, plus=1))
                if (v := upto(t, r, 6)) is not None:
                    dve.wait_ge(m_done, v)
                if (v := upto(t, r, 6)) is not None:
                    dve.wait_ge(mv2_done, v)
                dve.tensor_tensor(y_sb[:, k:k + 2], (B, C)[half][:, 0:2 * P].rearrange("p (s m) -> p s m", s=2),
                                  x1_sb[:, k:k + 2], ALU.add).then_inc(y_done, 1)

            def statistics(t, r, lag, src, st, mv, st_done, mv_done, mv_used):
                for s in range(SEQS):
                    ins = dve.bn_stats(st[:, s], src[:, s])
                ins.then_inc(st_done, 1)
                dve.wait_ge(st_done, upto(t, r, lag, plus=1))
                if (v := upto(t, r, lag)) is not None:
                    dve.wait_ge(mv_used, v)
                dve.memset(pause[:], 0.0)
                for s in range(SEQS):
                    ins = dve.bn_aggr(mv[:, s], st[:, s])
                ins.then_inc(mv_done, 1)

            def step(t, r):
                for u in range(UNITS):
                    if u in (0, 1) and live(t, r, 6):
                        add_y(t, r, u)
                    if u == 5 and live(t, r, 4):
                        normalise(t, r, 1)
                    if u == 7 and live(t, r, 4):
                        dve.wait_ge(wo_done, upto(t, r, 4, plus=1))
                        dve.wait_ge(xb_done, upto(t, r, 4, plus=1))
                        if (v := upto(t, r, 4)) is not None:
                            dve.wait_ge(n_done, v)
                        if (v := upto(t, r, 4)) is not None:
                            dve.wait_ge(mv1_done, v)
                        dve.tensor_tensor(z_sb[:], A[:].rearrange("p (s m) -> p s m", s=SEQS), xb_sb[:, (r - 4) % 4],
                                          ALU.add).then_inc(z_done, 1)
                    if live(t, r, 2):
                        n = UNITS * (r - 2) + u
                        s, half = u // 2, u % 2
                        dve.wait_ge(s_done, upto(t, r, 2, per=UNITS, plus=u + 1))
                        if (v := upto(t, r, 3)) is not None:
                            dve.wait_ge(maxT_done, v)
                        dve.reduce_max(max_sb[:, (r - 2) % 2, half * HU:(half + 1) * HU, s],
                                       s_ps[n % 2][:].rearrange("p (h k) -> p h k", h=HU), AX.X).then_inc(max_done, 1)
                    if u == 0 and live(t, r, 3):
                        mT = A[0:H * SEQS, 0:P]
                        dve.wait_ge(maxT_done, upto(t, r, 3, plus=1))
                        if (v := upto(t, r, 3, per=DMA)) is not None:
                            dve.wait_ge(max_written, v)
                        dve.tensor_scalar(max_parts[:, HI], mT, -1.0, None, ALU.mult).then_inc(max_hi, 1)
                        dve.wait_ge(max_hi, upto(t, r, 3, plus=1))
                        dve.scalar_tensor_tensor(max_rest[:], mT, -1.0, max_parts[:, HI],
                                                 ALU.mult, ALU.subtract).then_inc(max_rest_made, 1)
                        dve.wait_ge(max_rest_made, upto(t, r, 3, plus=1))
                        dve.tensor_copy(max_parts[:, MID], max_rest[:]).then_inc(max_mid, 1)
                        dve.wait_ge(max_mid, upto(t, r, 3, plus=1))
                        dve.tensor_tensor(max_parts[:, LO], max_rest[:], max_parts[:, MID],
                                          ALU.subtract).then_inc(max_parts_made, 1)
                    if u == 1 and live(t, r, 4):
                        normalise(t, r, 0)
                    if u == 1 and live(t, r, 5):
                        dve.wait_ge(rs1_done, upto(t, r, 5, plus=1))
                        if (v := upto(t, r, 5)) is not None:
                            dve.wait_ge(x1T_done, v)
                        if (v := upto(t, r, 5)) is not None:
                            dve.wait_ge(x1g_done, v)
                        for s in range(SEQS):
                            ins = dve.tensor_scalar(n_sb[:, s], z_sb[:, s], mv1[:, s, 0:1], rs1[:, s:s + 1],
                                                    ALU.subtract, ALU.mult)
                        ins.then_inc(n_done, 1)
                    if u in (2, 3) and live(t, r, 0):
                        split(t, r, u - 2)
                    if u == 4 and live(t, r, 6):
                        dve.wait_ge(y_done, upto(t, r, 6, per=2, plus=2))
                        statistics(t, r, 6, y_sb, st2, mv2, st2_done, mv2_done, m_done)
                    if u == 6 and live(t, r, 6):
                        dve.wait_ge(rs2_done, upto(t, r, 6, plus=1))
                        if (v := upto(t, r, 6)) is not None:
                            dve.wait_ge(mg_done, v)
                        for s in range(SEQS):
                            ins = dve.tensor_scalar(m_sb[:, s], y_sb[:, s], mv2[:, s, 0:1], rs2[:, s:s + 1],
                                                    ALU.subtract, ALU.mult)
                        ins.then_inc(m_done, 1)
                    if u == 7 and live(t, r, 4):
                        dve.wait_ge(z_done, upto(t, r, 4, plus=1))
                        statistics(t, r, 4, z_sb, st1, mv1, st1_done, mv1_done, n_done)

            iterate(dve, step, 2 * UNROLL, G, 6)

        @block.tensor
        def _(pe):
            pe.wait_ge(consts_loaded, N_CONST * DMA)
            pe.wait_ge(consts_set, 5)
            pe.wait_ge(bv_wide_set, 1)
            for s in range(SEQS):
                ins = pe.matmul(A[:, s * P:(s + 1) * P], bv_wide[:], wo_sb[:], start=True, stop=True)
            ins.then_inc(bv_wo_done, 1)
            pe.wait_ge(rows_set, 4)

            def transposes(bank, srcs):
                for k, src in enumerate(srcs):
                    ins = pe.transpose(bank[:, k * P:(k + 1) * P], src, ident[:])
                return ins

            def hidden(t, r, c):
                if c == 0:
                    pe.wait_ge(x1T_copied, upto(t, r, 5, plus=1))
                    pe.wait_ge(rest_made, upto(t, r, 0, per=2, plus=1))
                    if not live(t, r, 0):
                        pe.wait_ge(y_done, upto(t, r, 6, per=2, plus=1))
                elif c == 1:
                    pe.wait_ge(x1T_copied, upto(t, r, 5, plus=1))
                else:
                    pe.wait_ge(h_ready, upto(t, r, 5, per=FC, plus=c - 1))
                pe.matmul((B, C)[c % 2][:], w1_sb[:, c * P:(c + 1) * P], x1T_sb[:], start=True,
                          stop=True).then_inc(f1_done, 1)

            def down(t, r, lag, half):
                for s in range(2):
                    tok = slice((2 * half + s) * P, (2 * half + s + 1) * P)
                    for c in range(FC):
                        if s == 0:
                            pe.wait_ge(h_ready, upto(t, r, lag, per=FC, plus=max(c + 1, FC - 1)))
                        ins = pe.matmul((B, C)[half][:, s * P:(s + 1) * P], h_sb[:, c, tok], w2_sb[:, c],
                                        start=c == 0, stop=c == FC - 1)
                ins.then_inc(f2_done, 1)

            def o_back(t, r, half):
                pe.wait_ge(oT_copied, upto(t, r, 4, per=2, plus=half + 1))
                transposes(A, [oT_sb[:, half, k * P:(k + 1) * P] for k in range(4)]).then_inc(o_back_done, 1)

            def step(t, r):
                for u in range(UNITS):
                    if live(t, r, 2):
                        n, s = UNITS * (r - 2) + u, u // 2
                        tok = slice(s * P, (s + 1) * P)
                        if u == 0:
                            pe.wait_ge(stack_loaded[(r - 2) % 2], upto_dma(t, r, 2, per=6 * DMA))
                        if (v := upto(t, r, 2, per=UNITS, plus=u - 1)) is not None:
                            pe.wait_ge(max_done, v)
                        for j in range(HU):
                            h = HU * (u % 2) + j
                            ins = pe.matmul(s_ps[n % 2][:, j * P:(j + 1) * P], stack[0:PROD, (r - 2) % 4, 0, h, tok],
                                            stack[0:PROD, (r - 2) % 4, 1, h, tok], start=True, stop=True)
                        ins.then_inc(s_done, 1)
                    lag, unit = sT_unit(u)
                    if live(t, r, lag):
                        n, s = UNITS * (r - lag) + unit, unit // 2
                        tok = slice(s * P, (s + 1) * P)
                        if unit == 0:
                            pe.wait_ge(max_rows_loaded, upto(t, r, lag, per=DMA, plus=DMA))
                        if (v := upto(t, r, lag, per=UNITS, plus=unit - 1)) is not None:
                            pe.wait_ge(exp_done, v)
                        for j in range(HU):
                            h = HU * (unit % 2) + j
                            ins = pe.matmul(sT_ps[n % 2][:, j * P:(j + 1) * P], stack[:, (r - lag) % 4, 1, h, tok],
                                            stack[:, (r - lag) % 4, 0, h, tok], start=True, stop=True)
                        ins.then_inc(sT_done, 1)
                    if u == 0:
                        if live(t, r, 3):
                            pe.wait_ge(max_done, upto(t, r, 3, per=UNITS, plus=UNITS))
                            if (v := upto(t, r, 5, plus=1)) is not None:
                                pe.wait_ge(z_done, v)
                            pe.transpose(A[0:H * SEQS, 0:P], max_sb[:, (r - 3) % 2].rearrange("p h s -> p (h s)"),
                                         ident[:]).then_inc(maxT_done, 1)
                        if live(t, r, 6):
                            down(t, r, 6, 1)
                    if u == 1:
                        if live(t, r, 4):
                            if live(t, r, 3):
                                pe.wait_ge(max_rest_made, upto(t, r, 3, plus=1))
                            else:
                                pe.wait_ge(z_done, upto(t, r, 5, plus=1))
                            o_back(t, r, 0)
                        if live(t, r, 0):
                            pe.wait_ge(x_loaded[r % 2], upto_dma(t, r, 0))
                            if (v := upto(t, r, 6, per=2, plus=2)) is not None:
                                pe.wait_ge(y_done, v)
                            transposes(C, [x_sb[:, r % 2, s] for s in range(SEQS)]).then_inc(xT_done, 1)
                    if u == 2:
                        if live(t, r, 0):
                            pe.wait_ge(xT_copied, upto(t, r, 0, plus=1))
                            if (v := upto(t, r, 6, per=2, plus=1)) is not None:
                                pe.wait_ge(y_done, v)
                            elif (v := upto(t, r, 0, per=2)) is not None:
                                pe.wait_ge(rest_made, v)
                            pe.matmul(B[:], wq_sb[:], xT_sb[:, r % 2], start=True, stop=True).then_inc(q_done, 1)
                        if live(t, r, 1):
                            if live(t, r, 4):
                                pe.wait_ge(o_normed, upto(t, r, 4, per=2, plus=1))
                            elif live(t, r, 3):
                                pe.wait_ge(max_rest_made, upto(t, r, 3, plus=1))
                            else:
                                pe.wait_ge(rest_made, upto(t, r, 1, per=2, plus=2))
                            for s in range(SEQS):
                                ins = pe.matmul(A[:, s * P:(s + 1) * P], xT_sb[:, (r - 1) % 2, s * P:(s + 1) * P],
                                                wv_sb[:], start=True, stop=True)
                            ins.then_inc(v_done, 1)
                        if live(t, r, 5):
                            pe.wait_ge(n_done, upto(t, r, 5, plus=1))
                            pe.wait_ge(xT_copied, upto(t, r, 0, plus=1))
                            if not live(t, r, 0):
                                pe.wait_ge(y_done, upto(t, r, 6, per=2, plus=2))
                            transposes(C, [n_sb[:, s] for s in range(SEQS)]).then_inc(x1T_done, 1)
                    if u == 3:
                        if live(t, r, 0):
                            if (v := upto(t, r, 1, plus=1)) is not None:
                                pe.wait_ge(v_copied, v)
                            pe.matmul(A[:], wk_sb[:], xT_sb[:, r % 2], start=True, stop=True).then_inc(k_done, 1)
                        if live(t, r, 5):
                            hidden(t, r, 0)
                    if u == 4:
                        if live(t, r, 5):
                            hidden(t, r, 1)
                        if live(t, r, 4):
                            pe.wait_ge(rest_made, upto(t, r, 0, per=2, plus=2))
                            if not live(t, r, 0):
                                pe.wait_ge(v_copied, upto(t, r, 1, plus=1))
                                pe.wait_ge(o_normed, upto(t, r, 4, per=2, plus=1))
                            o_back(t, r, 1)
                    if u == 5:
                        if live(t, r, 5):
                            hidden(t, r, 2)
                        if live(t, r, 4):
                            pe.wait_ge(o_normed, upto(t, r, 4, per=2, plus=2))
                            transposes(A, [o_sb[:, s] for s in range(SEQS)]).then_inc(onT_done, 1)
                    if u == 6:
                        if live(t, r, 5):
                            hidden(t, r, 3)
                        if live(t, r, 4):
                            pe.wait_ge(onT_copied, upto(t, r, 4, plus=1))
                            for s in range(SEQS):
                                ins = pe.matmul(A[:, s * P:(s + 1) * P], onT_sb[:, s * P:(s + 1) * P], wo_sb[:],
                                                start=True, stop=True)
                            ins.then_inc(wo_done, 1)
                    if u == 7 and live(t, r, 5):
                        down(t, r, 5, 0)
                    lag, unit = sT_unit(u)
                    if live(t, r, lag):
                        n, s = UNITS * (r - lag) + unit, unit // 2
                        pe.wait_ge(exp_done, upto(t, r, lag, per=UNITS, plus=unit + 1))
                        if unit == 0:
                            pe.wait_ge(v_copied, upto(t, r, lag, plus=1))
                        if unit % 4 == 0:
                            if (v := upto(t, r, lag, per=2, plus=unit // 4)) is not None:
                                pe.wait_ge(oT_copied, v)
                        for j in range(HU):
                            h = HU * (unit % 2) + j
                            ins = pe.matmul(oT_ps[j * VW:(j + 1) * VW, (unit % 4) * P:(unit % 4 + 1) * P],
                                            v_ones[:, (r - lag) % 4, s, h], prob_sb[:, n % 4, j * P:(j + 1) * P],
                                            start=True, stop=True)
                        ins.then_inc(pv_done, 1)

            iterate(pe, step, 2 * UNROLL, G, 6)


NAMES = ["wq", "bq", "wk", "bk", "wv", "bv", "wo", "bo", "w1", "b1", "w2", "b2", "ln1_g", "ln1_b", "ln2_g", "ln2_b"]


def kernel(**inputs):
    import numpy as _np
    import concourse.bacc as _bacc
    from concourse import mybir as _mybir
    from concourse.bass_utils import run_bass_kernel_spmd as _run

    nc = _bacc.Bacc("TRN2", target_bir_lowering=False, num_devices=1)
    arrays, args = {}, []
    for name in ["x"] + ["L0_conv_" + n for n in NAMES]:
        a = _np.ascontiguousarray(inputs[name])
        arrays[f"in_{name}"] = a
        args.append(nc.dram_tensor(f"in_{name}", a.shape, _mybir.dt.from_np(a.dtype), kind="ExternalInput").ap())
    out = nc.dram_tensor("out", arrays["in_x"].shape, F32, kind="ExternalOutput").ap()
    build(nc, *args, out)
    return _run(nc, [arrays], core_ids=[0]).results[0]["out"]
```

```python
import concourse.bass as bass
from concourse import mybir
from contextlib import ExitStack

F32 = mybir.dt.float32
BF16 = mybir.dt.bfloat16
F32R = mybir.dt.float32r
ALU = mybir.AluOpType
ACT = mybir.ActivationFunctionType
AX = mybir.AxisListType

P = 128
H, D = 8, 16
SEQS = 4
T = SEQS * P
FF = 512
FC = FF // P
HU = 4
UNITS = SEQS * H // HU
VW = 32
EPS = 1e-5
HI, MID, LO = range(3)
REST = 1
Q_PARTS = (HI, HI, HI, MID, MID, LO)
K_PARTS = (HI, MID, LO, HI, MID, HI)
PROD = len(Q_PARTS) * D
STACK_DMAS = 2 * len(Q_PARTS)
MAXROWS = 3
UNROLL = 4
DMA = 16


def build(nc, x, wq, bq, wk, bk, wv, bv, wo, bo, w1, b1, w2, b2, g1, be1, g2, be2, out):
    n_seq = x.shape[0] * x.shape[1]
    G = n_seq // SEQS
    assert G % UNROLL == 0 and G >= 4 * UNROLL
    x_g = x.rearrange("b r k m -> (b r) k m").rearrange("(g s) k m -> g k s m", s=SEQS)
    out_g = out.rearrange("b r k m -> (b r) k m").rearrange("(g s) k m -> g k s m", s=SEQS)

    with ExitStack() as ctx:
        def sb(name, shape, dt=F32):
            return ctx.enter_context(nc.sbuf_tensor(name, shape, dt))

        def sem(name):
            return ctx.enter_context(nc.semaphore(name))

        wq_in, wk_in = sb("wq_in", [P, H, D]), sb("wk_in", [P, H, D])
        wq_parts, wk_parts = sb("wq_parts", [P, 2, P], F32R), sb("wk_parts", [P, 2, P], F32R)
        wv_sb, wo_sb = sb("wv_sb", [P, P]), sb("wo_sb", [P, P])
        w1_sb, w2_sb = sb("w1_sb", [P, FF]), sb("w2_sb", [P, FC, P])
        w1g_sb, w1_parts = sb("w1g_sb", [P, FF]), sb("w1_parts", [P, 2, FF], F32R)
        bq_col, bk_col, bv_col, g1_col, be1_col = (sb(n, [P, 1]) for n in ("bq_col", "bk_col", "bv_col", "g1_col", "be1_col"))
        b1_col = sb("b1_col", [P, FC])
        bo_row, b2_row = sb("bo_row", [P, SEQS, P]), sb("b2_row", [P, SEQS, P])
        be1_row, g1_row = sb("be1_row", [P, SEQS, P]), sb("g1_row", [P, SEQS, P])
        g2_row, be2_row = sb("g2_row", [P, SEQS, P]), sb("be2_row", [P, SEQS, P])
        bv_wide, ident = sb("bv_wide", [P, P]), sb("ident", [P, P])
        minus_half, minus_one, eps_sb = (sb(n, [P, SEQS]) for n in ("minus_half", "minus_one", "eps_sb"))
        pause = sb("pause", [P, 1])
        x_sb = sb("x_sb", [P, 2, SEQS, P])
        xb_sb = sb("xb_sb", [P, 4, SEQS, P])
        xT_sb, xT_parts = sb("xT_sb", [P, 2, T]), sb("xT_parts", [P, 2, T], F32R)
        parts = sb("parts", [P, 2, 6, T], BF16)
        rest_sb = sb("rest_sb", [P, 2, T])
        stack = sb("stack", [PROD + MAXROWS, 4, 2, H, T], BF16)
        v_ones = sb("v_ones", [P, 4, SEQS, H, VW])
        max_sb = sb("max_sb", [P, 2, H, SEQS])
        max_parts = sb("max_parts", [H * SEQS, MAXROWS, P], BF16)
        max_rest = sb("max_rest", [H * SEQS, P])
        prob_sb = sb("prob_sb", [P, 4, HU * P])
        oT_sb = sb("oT_sb", [P, 2, HU * P])
        recip = sb("recip", [P, 4, HU])
        o_sb = sb("o_sb", [P, SEQS, P])
        onT_sb = sb("onT_sb", [P, T])
        z_sb, n_sb, x1_sb = sb("z_sb", [P, SEQS, P]), sb("n_sb", [P, SEQS, P]), sb("x1_sb", [P, SEQS, P])
        x1g_sb = sb("x1g_sb", [P, SEQS, P])
        nT_parts = sb("nT_parts", [P, 2, T], F32R)
        h_sb = sb("h_sb", [P, FC, T])
        y_sb, m_sb, mg_sb = sb("y_sb", [P, SEQS, P]), sb("m_sb", [P, SEQS, P]), sb("mg_sb", [P, SEQS, P])
        out_sb = sb("out_sb", [P, 2, SEQS, P])
        st1, mv1, ve1, rs1, minus_m1, shift1 = sb("st1", [P, SEQS, 6]), sb("mv1", [P, SEQS, 2]), sb("ve1", [P, SEQS]), *(sb(n, [P, SEQS]) for n in ("rs1", "minus_m1", "shift1"))
        st2, mv2, ve2, rs2, minus_m2, shift2 = sb("st2", [P, SEQS, 6]), sb("mv2", [P, SEQS, 2]), sb("ve2", [P, SEQS]), *(sb(n, [P, SEQS]) for n in ("rs2", "minus_m2", "shift2"))
        s_ps = [ctx.enter_context(nc.psum_tensor(f"s_ps{b}", [P, T], F32)) for b in range(2)]
        sT_ps = [ctx.enter_context(nc.psum_tensor(f"sT_ps{b}", [P, T], F32)) for b in range(2)]
        oT_ps, A, B, C = (ctx.enter_context(nc.psum_tensor(n, [P, T], F32)) for n in ("oT_ps", "bankA", "bankB", "bankC"))

        qk_loaded, qk_made, consts_loaded = sem("qk_loaded"), sem("qk_made"), sem("consts_loaded")
        ident_zero, ident_set, consts_set = sem("ident_zero"), sem("ident_set"), sem("consts_set")
        stack_ones_set = sem("stack_ones_set")
        bv_wide_set, w_products_done, consts_made = sem("bv_wide_set"), sem("w_products_done"), sem("consts_made")
        w1g_set, w_hi_set = sem("w1g_set"), sem("w_hi_set")
        x_loaded = [sem("x_loaded0"), sem("x_loaded1")]
        stack_loaded = [sem("stack_loaded0"), sem("stack_loaded1")]
        max_rows_loaded = sem("max_rows_loaded")
        out_stored = [sem("out_stored0"), sem("out_stored1")]
        xT_done, q_done, k_done, v_done = sem("xT_done"), sem("q_done"), sem("k_done"), sem("v_done")
        s_done, maxT_done, sT_done, pv_done = sem("s_done"), sem("maxT_done"), sem("sT_done"), sem("pv_done")
        o_back_done, onT_done, wo_done = sem("o_back_done"), sem("onT_done"), sem("wo_done")
        nT_done, f1_done, f2_done = sem("nT_done"), sem("f1_done"), sem("f2_done")
        xT_hi, hi_split, v_copied, exp_done = sem("xT_hi"), sem("hi_split"), sem("v_copied"), sem("exp_done")
        oT_copied, onT_copied, nT_hi, h_ready = sem("oT_copied"), sem("onT_copied"), sem("nT_hi"), sem("h_ready")
        n_done, m_done = sem("n_done"), sem("m_done")
        rest_made, mid_split, max_done, nT_lo, xT_lo = sem("rest_made"), sem("mid_split"), sem("max_done"), sem("nT_lo"), sem("xT_lo")
        max_hi, max_rest_made, max_mid, max_parts_made = sem("max_hi"), sem("max_rest_made"), sem("max_mid"), sem("max_parts_made")
        recip_made, o_normed = sem("recip_made"), sem("o_normed")
        z_done, st1_done, mv1_done = sem("z_done"), sem("st1_done"), sem("mv1_done")
        y_done, st2_done, mv2_done = sem("y_done"), sem("st2_done"), sem("mv2_done")
        xb_done, lo_split, ve1_done, rs1_done = sem("xb_done"), sem("lo_split"), sem("ve1_done"), sem("rs1_done")
        x1g_done, x1_done, ve2_done, rs2_done = sem("x1g_done"), sem("x1_done"), sem("ve2_done"), sem("rs2_done")
        shift1_done, shift2_done = sem("shift1_done"), sem("shift2_done")
        xT_joined, mg_done, out_ready = sem("xT_joined"), sem("mg_done"), sem("out_ready")

        def live(t, r, lag):
            return not isinstance(t, int) or 0 <= r - lag < G

        def upto(t, r, lag, per=1, plus=0):
            plus += per * (r - lag)
            if isinstance(t, int):
                return min(plus, per * G) if plus > 0 else None
            return t * per + plus if plus else t * per

        def upto_dma(t, r, lag, before=0, per=DMA):
            plus = per * ((r - lag) // 2 + 1 - before)
            if isinstance(t, int):
                return plus if plus > 0 else None
            return t * (per // 2) + plus if plus else t * (per // 2)

        def sT_unit(u):
            return (4, u + 4) if u < 4 else (3, u - 4)

        def iterate(eng, step, begin, first, last, lags):
            for r in range(begin, first):
                step(0, r)
            with eng.Fori(first, last, UNROLL) as t:
                for r in range(UNROLL):
                    step(t, r)
            for r in range(last, G + lags):
                step(0, r)

        N_QK, N_CONST, N_SET, N_MADE = 4, 14, 4, 4
        block = ctx.enter_context(nc.Block())

        @block.sync
        def _(sp):
            def row(v):
                return v.rearrange("(a b m) -> a b m", a=1, b=1).broadcast_to([P, SEQS, P])

            def col(v):
                return v.rearrange("(p a) -> p a", a=1)

            def by_feature(v):
                return v.rearrange("(h d a) -> d h a", h=H, a=1)

            sp.dma_start(x_sb[:, 0], x_g[0]).then_inc(x_loaded[0], DMA)
            for dst, src in ((wq_in[:].rearrange("p h d -> p (h d)"), wq), (wk_in[:].rearrange("p h d -> p (h d)"), wk),
                             (bq_col[:], by_feature(bq)), (bk_col[:], by_feature(bk))):
                sp.dma_start(dst, src, allow_slow_non_contiguous=True).then_inc(qk_loaded, DMA)
            for dst, src in ((wv_sb[:], wv), (wo_sb[:], wo), (w1_sb[:], w1),
                             (w2_sb[:], w2.rearrange("(c p) m -> p c m", p=P)), (bv_col[:], col(bv)),
                             (g1_col[:], col(g1)), (be1_col[:], col(be1)),
                             (b1_col[:], b1.rearrange("(c p) -> p c", p=P)),
                             (bo_row[:], row(bo)), (b2_row[:], row(b2)), (be1_row[:], row(be1)),
                             (g1_row[:], row(g1)), (g2_row[:], row(g2)), (be2_row[:], row(be2))):
                sp.dma_start(dst, src, allow_slow_non_contiguous=True).then_inc(consts_loaded, DMA)

            def step(t, r):
                if live(t, r, 3):
                    sp.wait_ge(max_parts_made, upto(t, r, 3, plus=1))
                    for part in range(MAXROWS):
                        sp.dma_start(stack[PROD + part:PROD + part + 1, (r - 3) % 4, 0],
                                     max_parts[:, part]).then_inc(max_rows_loaded, DMA)
                if live(t, r, -1):
                    if (v := upto(t, r, 0)) is not None:
                        sp.wait_ge(xT_done, v)
                    if (v := upto(t, r, 0)) is not None:
                        sp.wait_ge(xb_done, v)
                    sp.dma_start(x_sb[:, (r + 1) % 2], x_g[t + (r + 1)]).then_inc(x_loaded[(r + 1) % 2], DMA)
                if live(t, r, 7):
                    sp.wait_ge(out_ready, upto(t, r, 7, plus=1))
                    sp.dma_start(out_g[t + (r - 7)], out_sb[:, (r - 7) % 2]).then_inc(out_stored[(r - 7) % 2], DMA)
                if live(t, r, 0):
                    sp.wait_ge(lo_split, upto(t, r, 0, per=2, plus=2))
                    for j in range(len(Q_PARTS)):
                        for c, part in enumerate((Q_PARTS[j], K_PARTS[j])):
                            sp.dma_start(stack[j * D:(j + 1) * D, r % 4, c].rearrange("d h x -> d (h x)"),
                                         parts[:, r % 2, 3 * c + part]).then_inc(stack_loaded[r % 2], DMA)

            iterate(sp, step, 0, 2 * UNROLL, G - UNROLL, 7)
            sp.wait_ge(out_stored[(G - 2) % 2], upto_dma(0, G - 2, 0))
            sp.wait_ge(out_stored[(G - 1) % 2], upto_dma(0, G - 1, 0))

        @block.gpsimd
        def _(pool):
            pool.memset(ident[:], 0.0).then_inc(ident_zero, 1)
            pool.wait_ge(ident_zero, 1)
            pool.affine_select(out=ident[:], in_=ident[:], compare_op=ALU.not_equal, fill=1.0, base=0,
                               pattern=[[-1, P]], channel_multiplier=1).then_inc(ident_set, 1)
            pool.memset(v_ones[:], 1.0).then_inc(consts_set, 1)
            pool.memset(minus_half[:], -0.5).then_inc(consts_set, 1)
            pool.memset(minus_one[:], -1.0).then_inc(consts_set, 1)
            pool.memset(eps_sb[:], EPS).then_inc(consts_set, 1)
            pool.wait_ge(consts_set, N_SET)
            pool.memset(stack[PROD:PROD + MAXROWS, 0:2, 1], 1.0).then_inc(stack_ones_set, 1)

            def lo_part(t, r, c):
                pool.wait_ge(mid_split, upto(t, r, 0, per=2, plus=c + 1))
                if (v := upto_dma(t, r, 0, before=1, per=STACK_DMAS * DMA)) is not None:
                    pool.wait_ge(stack_loaded[r % 2], v)
                pool.tensor_tensor(parts[:, r % 2, 3 * c + LO], rest_sb[:, c], parts[:, r % 2, 3 * c + MID],
                                   ALU.subtract).then_inc(lo_split, 1)

            def step(t, r):
                if live(t, r, 1):
                    pool.wait_ge(x_loaded[(r - 1) % 2], upto_dma(t, r, 1))
                    if (v := upto(t, r, 5, plus=1)) is not None:
                        pool.wait_ge(z_done, v)
                    pool.tensor_tensor(xb_sb[:, (r - 1) % 4], x_sb[:, (r - 1) % 2], bo_row[:],
                                       ALU.add).then_inc(xb_done, 1)
                if live(t, r, 5):
                    pool.wait_ge(n_done, upto(t, r, 5, plus=1))
                    if (v := upto(t, r, 5)) is not None:
                        pool.wait_ge(x1_done, v)
                    pool.tensor_tensor(x1g_sb[:], n_sb[:], g1_row[:], ALU.mult).then_inc(x1g_done, 1)
                    pool.wait_ge(x1g_done, upto(t, r, 5, plus=1))
                    if (v := upto(t, r, 5, per=2)) is not None:
                        pool.wait_ge(y_done, v)
                    pool.tensor_tensor(x1_sb[:], x1g_sb[:], be1_row[:], ALU.add).then_inc(x1_done, 1)
                if live(t, r, 0):
                    lo_part(t, r, 0)
                if live(t, r, 0):
                    lo_part(t, r, 1)
                    pool.wait_ge(xT_lo, upto(t, r, 0, plus=1))
                    if (v := upto(t, r, 1)) is not None:
                        pool.wait_ge(v_done, v)
                    pool.tensor_tensor(xT_sb[:, r % 2], xT_parts[:, HI].bitcast(F32), xT_parts[:, REST].bitcast(F32),
                                       ALU.add).then_inc(xT_joined, 1)
                if live(t, r, 6):
                    pool.wait_ge(mv2_done, upto(t, r, 6, plus=1))
                    if (v := upto(t, r, 6)) is not None:
                        pool.wait_ge(m_done, v)
                    pool.tensor_tensor(minus_m2[:], mv2[:, :, 0], minus_one[:], ALU.mult)
                    pool.tensor_tensor(ve2[:], mv2[:, :, 1], eps_sb[:], ALU.add).then_inc(ve2_done, 1)
                    pool.wait_ge(ve2_done, upto(t, r, 6, plus=1))
                    pool.tensor_tensor(rs2[:], ve2[:], minus_half[:], ALU.pow).then_inc(rs2_done, 1)
                    pool.wait_ge(rs2_done, upto(t, r, 6, plus=1))
                    pool.tensor_tensor(shift2[:], minus_m2[:], rs2[:], ALU.mult).then_inc(shift2_done, 1)
                if live(t, r, 4):
                    pool.wait_ge(mv1_done, upto(t, r, 4, plus=1))
                    if (v := upto(t, r, 4)) is not None:
                        pool.wait_ge(n_done, v)
                    pool.tensor_tensor(minus_m1[:], mv1[:, :, 0], minus_one[:], ALU.mult)
                    pool.tensor_tensor(ve1[:], mv1[:, :, 1], eps_sb[:], ALU.add).then_inc(ve1_done, 1)
                    pool.wait_ge(ve1_done, upto(t, r, 4, plus=1))
                    pool.tensor_tensor(rs1[:], ve1[:], minus_half[:], ALU.pow).then_inc(rs1_done, 1)
                    pool.wait_ge(rs1_done, upto(t, r, 4, plus=1))
                    pool.tensor_tensor(shift1[:], minus_m1[:], rs1[:], ALU.mult).then_inc(shift1_done, 1)
                if live(t, r, 6):
                    pool.wait_ge(m_done, upto(t, r, 6, plus=1))
                    if (v := upto(t, r, 6)) is not None:
                        pool.wait_ge(out_ready, v)
                    pool.tensor_tensor(mg_sb[:], m_sb[:], g2_row[:], ALU.mult).then_inc(mg_done, 1)
                    pool.wait_ge(mg_done, upto(t, r, 6, plus=1))
                    if (v := upto_dma(t, r, 6, before=1)) is not None:
                        pool.wait_ge(out_stored[(r - 6) % 2], v)
                    pool.tensor_tensor(out_sb[:, (r - 6) % 2], mg_sb[:], be2_row[:], ALU.add).then_inc(out_ready, 1)

            pool.wait_ge(stack_ones_set, 1)
            step(0, 0)
            pool.wait_ge(xT_joined, 1)
            pool.memset(stack[PROD:PROD + MAXROWS, 2:4, 1], 1.0).then_inc(stack_ones_set, 1)
            pool.wait_ge(stack_ones_set, 2)
            pool.wait_ge(consts_loaded, N_CONST * DMA)
            pool.wait_ge(consts_made, N_MADE)
            iterate(pool, step, 1, 2 * UNROLL, G, 6)

        @block.scalar
        def _(act):
            act.wait_ge(qk_loaded, N_QK * DMA)

            def hi_part(t, r, c):
                act.wait_ge((q_done, k_done)[c], upto(t, r, 0, plus=1))
                if (v := upto_dma(t, r, 0, before=1, per=STACK_DMAS * DMA)) is not None:
                    act.wait_ge(stack_loaded[r % 2], v)
                act.activation(parts[:, r % 2, 3 * c + HI], (B, A)[c][:], ACT.Identity,
                               bias=(bq_col, bk_col)[c][:]).then_inc(hi_split, 1)

            def relu(t, r, c):
                act.wait_ge(f1_done, upto(t, r, 5, per=FC, plus=c + 1))
                if (v := upto(t, r, 5, per=2)) is not None:
                    act.wait_ge(f2_done, v)
                act.activation(h_sb[:, c], (C, B)[c % 2][:], ACT.Relu, bias=b1_col[:, c:c + 1]).then_inc(h_ready, 1)

            def copy_oT(t, r, lag, half):
                act.wait_ge(pv_done, upto(t, r, lag, per=UNITS, plus=4 * half + 4))
                if (v := upto(t, r, lag, per=2, plus=half - 1)) is not None:
                    act.wait_ge(o_back_done, v)
                act.activation(oT_sb[:, half], oT_ps[:], ACT.Copy).then_inc(oT_copied, 1)

            def copy_onT(t, r):
                act.wait_ge(onT_done, upto(t, r, 4, plus=1))
                if (v := upto(t, r, 4)) is not None:
                    act.wait_ge(wo_done, v)
                act.activation(onT_sb[:], A[:], ACT.Copy).then_inc(onT_copied, 1)

            def step(t, r):
                for u in range(UNITS):
                    if u == 0 and live(t, r, 4):
                        copy_oT(t, r, 4, 0)
                    if u == 4 and live(t, r, 4):
                        copy_oT(t, r, 4, 1)
                    lag, unit = sT_unit(u)
                    if live(t, r, lag):
                        n = (UNITS * (r - lag) + unit)
                        act.wait_ge(sT_done, upto(t, r, lag, per=UNITS, plus=unit + 1))
                        if (v := upto(t, r, lag, per=UNITS, plus=unit - 3)) is not None:
                            act.wait_ge(pv_done, v)
                        act.activation(prob_sb[:, n % 4], sT_ps[n % 2][:], ACT.Exp,
                                       scale=float(D) ** -0.5).then_inc(exp_done, 1)
                    if u == 0 and live(t, r, 5):
                        act.wait_ge(shift1_done, upto(t, r, 5, plus=1))
                        if (v := upto(t, r, 5)) is not None:
                            act.wait_ge(nT_done, v)
                        if (v := upto(t, r, 5)) is not None:
                            act.wait_ge(x1g_done, v)
                        for s in range(SEQS):
                            ins = act.activation(n_sb[:, s], z_sb[:, s], ACT.Identity, bias=shift1[:, s:s + 1],
                                                 scale=rs1[:, s:s + 1])
                        ins.then_inc(n_done, 1)
                    if u == 7 and live(t, r, 6):
                        act.wait_ge(shift2_done, upto(t, r, 6, plus=1))
                        if (v := upto(t, r, 6)) is not None:
                            act.wait_ge(mg_done, v)
                        for s in range(SEQS):
                            ins = act.activation(m_sb[:, s], y_sb[:, s], ACT.Identity, bias=shift2[:, s:s + 1],
                                                 scale=rs2[:, s:s + 1])
                        ins.then_inc(m_done, 1)
                    if u == 1 and live(t, r, 0):
                        act.wait_ge(xT_done, upto(t, r, 0, plus=1))
                        if (v := upto(t, r, 0)) is not None:
                            act.wait_ge(k_done, v)
                        if (v := upto(t, r, 0)) is not None:
                            act.wait_ge(xT_joined, v)
                        act.activation(xT_parts[:, HI], C[:], ACT.Copy).then_inc(xT_hi, 1)
                    if u == 2 and live(t, r, 1):
                        act.wait_ge(v_done, upto(t, r, 1, plus=1))
                        if (v := upto(t, r, 4, per=UNITS)) is not None:
                            act.wait_ge(pv_done, v)
                        act.activation(v_ones[:, (r - 1) % 4, :, :, 0:D],
                                       A[:].rearrange("p (s h d) -> p s h d", s=SEQS, h=H),
                                       ACT.Copy).then_inc(v_copied, 1)
                    if u == 2 and live(t, r, 5):
                        act.wait_ge(nT_done, upto(t, r, 5, plus=1))
                        if (v := upto(t, r, 5, per=FC)) is not None:
                            act.wait_ge(f1_done, v)
                        act.activation(nT_parts[:, HI], C[:], ACT.Copy).then_inc(nT_hi, 1)
                    if u == 2 and live(t, r, 0):
                        hi_part(t, r, 0)
                    if u == 3 and live(t, r, 0):
                        hi_part(t, r, 1)
                    if u in (3, 4, 5, 6) and live(t, r, 5):
                        relu(t, r, u - 3)
                    if u == 5 and live(t, r, 4):
                        copy_onT(t, r)

            step(0, 0)
            act.wait_ge(consts_loaded, N_CONST * DMA)
            act.wait_ge(consts_set, N_SET)
            step(0, 1)
            act.wait_ge(consts_made, N_MADE)
            iterate(act, step, 2, 2 * UNROLL, G, 6)

        @block.vector
        def _(dve):
            dve.wait_ge(qk_loaded, N_QK * DMA)
            for k, (w_parts, w_in) in enumerate(((wq_parts, wq_in), (wk_parts, wk_in))):
                w_hi, w_rest = (w_parts[:, part].rearrange("p (d h) -> p h d", h=H) for part in (HI, REST))
                dve.tensor_copy(w_hi, w_in[:]).then_inc(w_hi_set, 1)
                dve.wait_ge(w_hi_set, k + 1)
                dve.tensor_tensor(w_rest, w_in[:], w_hi.bitcast(F32), ALU.subtract).then_inc(qk_made, 1)

            def rest(t, r, c):
                dve.wait_ge(hi_split, upto(t, r, 0, per=2, plus=c + 1))
                if (v := upto(t, r, 0, per=2, plus=c - 1)) is not None:
                    dve.wait_ge(lo_split, v)
                dve.scalar_tensor_tensor(rest_sb[:, c], (B, A)[c][:], (bq_col, bk_col)[c][:],
                                         parts[:, r % 2, 3 * c + HI], ALU.add, ALU.subtract).then_inc(rest_made, 1)

            def mid(t, r, c):
                dve.wait_ge(rest_made, upto(t, r, 0, per=2, plus=c + 1))
                if (v := upto_dma(t, r, 0, before=1, per=STACK_DMAS * DMA)) is not None:
                    dve.wait_ge(stack_loaded[r % 2], v)
                dve.tensor_copy(parts[:, r % 2, 3 * c + MID], rest_sb[:, c]).then_inc(mid_split, 1)

            def normalise(t, r, half):
                o = A[:].rearrange("p (c w) -> p c w", w=VW)
                k = 2 * half
                dve.wait_ge(o_back_done, upto(t, r, 4, per=2, plus=half + 1))
                if (v := upto(t, r, 4, per=2, plus=half)) is not None:
                    dve.wait_ge(o_normed, v)
                dve.reciprocal(recip[:].rearrange("p c h -> p (c h)"), o[:, :, D]).then_inc(recip_made, 1)
                dve.wait_ge(recip_made, upto(t, r, 4, per=2, plus=half + 1))
                if (v := upto(t, r, 4)) is not None:
                    dve.wait_ge(onT_done, v)
                dve.tensor_tensor(o_sb[:, k:k + 2].rearrange("p s (h d) -> p (s h) d", d=D), o[:, :, 0:D],
                                  recip[:].rearrange("p c h -> p (c h)").unsqueeze(2).broadcast_to([P, 16, D]),
                                  ALU.mult).then_inc(o_normed, 1)

            def add_y(t, r, half):
                k = 2 * half
                dve.wait_ge(f2_done, upto(t, r, 6, per=2, plus=half + 1))
                dve.wait_ge(x1_done, upto(t, r, 6, plus=1))
                if (v := upto(t, r, 6)) is not None:
                    dve.wait_ge(m_done, v)
                if (v := upto(t, r, 6)) is not None:
                    dve.wait_ge(mv2_done, v)
                dve.tensor_tensor(y_sb[:, k:k + 2], (C, B)[half][:, 0:2 * P].rearrange("p (s m) -> p s m", s=2),
                                  x1_sb[:, k:k + 2], ALU.add).then_inc(y_done, 1)

            def statistics(t, r, lag, src, st, mv, st_done, mv_done, mv_used):
                for s in range(SEQS):
                    ins = dve.bn_stats(st[:, s], src[:, s])
                ins.then_inc(st_done, 1)
                dve.wait_ge(st_done, upto(t, r, lag, plus=1))
                if (v := upto(t, r, lag)) is not None:
                    dve.wait_ge(mv_used, v)
                dve.memset(pause[:], 0.0)
                for s in range(SEQS):
                    ins = dve.bn_aggr(mv[:, s], st[:, s])
                ins.then_inc(mv_done, 1)

            def step(t, r):
                for u in range(UNITS):
                    if u in (0, 1) and live(t, r, 6):
                        add_y(t, r, u)
                    if u == 3 and live(t, r, 0):
                        rest(t, r, 1)
                    if u == 5 and live(t, r, 4):
                        normalise(t, r, 1)
                    if u == 7 and live(t, r, 4):
                        dve.wait_ge(wo_done, upto(t, r, 4, plus=1))
                        dve.wait_ge(xb_done, upto(t, r, 4, plus=1))
                        if (v := upto(t, r, 4)) is not None:
                            dve.wait_ge(n_done, v)
                        if (v := upto(t, r, 4)) is not None:
                            dve.wait_ge(mv1_done, v)
                        dve.tensor_tensor(z_sb[:], A[:].rearrange("p (s m) -> p s m", s=SEQS), xb_sb[:, (r - 4) % 4],
                                          ALU.add).then_inc(z_done, 1)
                    if live(t, r, 2):
                        n = UNITS * (r - 2) + u
                        s, half = u // 2, u % 2
                        dve.wait_ge(s_done, upto(t, r, 2, per=UNITS, plus=u + 1))
                        if (v := upto(t, r, 3)) is not None:
                            dve.wait_ge(maxT_done, v)
                        dve.reduce_max(max_sb[:, (r - 2) % 2, half * HU:(half + 1) * HU, s],
                                       s_ps[n % 2][:].rearrange("p (h k) -> p h k", h=HU), AX.X).then_inc(max_done, 1)
                    if u == 0 and live(t, r, 3):
                        mT = A[0:H * SEQS, 0:P]
                        dve.wait_ge(maxT_done, upto(t, r, 3, plus=1))
                        if (v := upto(t, r, 3, per=MAXROWS * DMA)) is not None:
                            dve.wait_ge(max_rows_loaded, v)
                        dve.tensor_scalar(max_parts[:, HI], mT, -1.0, None, ALU.mult).then_inc(max_hi, 1)
                        dve.wait_ge(max_hi, upto(t, r, 3, plus=1))
                        dve.scalar_tensor_tensor(max_rest[:], mT, -1.0, max_parts[:, HI],
                                                 ALU.mult, ALU.subtract).then_inc(max_rest_made, 1)
                        dve.wait_ge(max_rest_made, upto(t, r, 3, plus=1))
                        dve.tensor_copy(max_parts[:, MID], max_rest[:]).then_inc(max_mid, 1)
                        dve.wait_ge(max_mid, upto(t, r, 3, plus=1))
                        dve.tensor_tensor(max_parts[:, LO], max_rest[:], max_parts[:, MID],
                                          ALU.subtract).then_inc(max_parts_made, 1)
                    if u == 1 and live(t, r, 4):
                        normalise(t, r, 0)
                    if u == 1 and live(t, r, 0):
                        dve.wait_ge(xT_hi, upto(t, r, 0, plus=1))
                        if (v := upto(t, r, 0)) is not None:
                            dve.wait_ge(k_done, v)
                        dve.tensor_tensor(xT_parts[:, REST], C[:], xT_parts[:, HI].bitcast(F32),
                                          ALU.subtract).then_inc(xT_lo, 1)
                    if u == 2 and live(t, r, 5):
                        dve.wait_ge(nT_hi, upto(t, r, 5, plus=1))
                        if (v := upto(t, r, 5, per=FC)) is not None:
                            dve.wait_ge(f1_done, v)
                        dve.tensor_tensor(nT_parts[:, REST], C[:], nT_parts[:, HI].bitcast(F32),
                                          ALU.subtract).then_inc(nT_lo, 1)
                    if u == 2 and live(t, r, 0):
                        rest(t, r, 0)
                        mid(t, r, 0)
                    if u == 3 and live(t, r, 0):
                        mid(t, r, 1)
                    if u == 5 and live(t, r, 6):
                        dve.wait_ge(y_done, upto(t, r, 6, per=2, plus=2))
                        statistics(t, r, 6, y_sb, st2, mv2, st2_done, mv2_done, m_done)
                    if u == 7 and live(t, r, 4):
                        dve.wait_ge(z_done, upto(t, r, 4, plus=1))
                        statistics(t, r, 4, z_sb, st1, mv1, st1_done, mv1_done, n_done)

            step(0, 0)
            dve.wait_ge(consts_loaded, N_CONST * DMA)
            dve.wait_ge(consts_set, N_SET)
            dve.wait_ge(ident_set, 1)
            dve.tensor_scalar(w1g_sb[:], w1_sb[:], g1_col[:], None, ALU.mult).then_inc(w1g_set, 1)
            dve.wait_ge(w1g_set, 1)
            dve.tensor_copy(w1_parts[:, HI], w1g_sb[:]).then_inc(w_hi_set, 1)
            dve.wait_ge(w_hi_set, 3)
            dve.tensor_tensor(w1_parts[:, REST], w1g_sb[:], w1_parts[:, HI].bitcast(F32), ALU.subtract).then_inc(consts_made, 1)
            dve.tensor_scalar(bv_wide[:], ident[:], 0.0, bv_col[:], ALU.mult, ALU.add).then_inc(bv_wide_set, 1)
            dve.tensor_tensor(be1_row[:], be1_row[:], b2_row[:], ALU.add).then_inc(consts_made, 1)
            dve.wait_ge(w_products_done, 2)
            dve.tensor_tensor(bo_row[:], s_ps[0][:].rearrange("p (s m) -> p s m", s=SEQS), bo_row[:],
                              ALU.add).then_inc(consts_made, 1)
            dve.tensor_tensor(b1_col[:], s_ps[1][:, 0:FC], b1_col[:], ALU.add).then_inc(consts_made, 1)
            iterate(dve, step, 1, 2 * UNROLL, G, 6)

        @block.tensor
        def _(pe):
            pe.wait_ge(ident_set, 1)
            pe.wait_ge(qk_made, 2)

            def transposes(bank, srcs):
                for k, src in enumerate(srcs):
                    ins = pe.transpose(bank[:, k * P:(k + 1) * P], src, ident[:])
                return ins

            def three_products(bank, w, xs):
                for k, (a, b) in enumerate(((HI, HI), (HI, REST), (REST, HI))):
                    ins = pe.matmul(bank, w[:, a], xs[:, b], start=k == 0, stop=k == 2)
                return ins

            def hidden(t, r, c):
                if c == 0:
                    pe.wait_ge(nT_lo, upto(t, r, 5, plus=1))
                elif c == 1:
                    pe.wait_ge(rest_made, upto(t, r, 0, per=2, plus=1))
                    if not live(t, r, 0) and (v := upto(t, r, 6, per=2, plus=2)) is not None:
                        pe.wait_ge(y_done, v)
                else:
                    pe.wait_ge(h_ready, upto(t, r, 5, per=FC, plus=c - 1))
                three_products((C, B)[c % 2][:], w1_parts[:, :, c * P:(c + 1) * P], nT_parts).then_inc(f1_done, 1)

            def down(t, r, lag, half):
                for s in range(2):
                    tok = slice((2 * half + s) * P, (2 * half + s + 1) * P)
                    for c in range(FC):
                        if s == 0:
                            pe.wait_ge(h_ready, upto(t, r, lag, per=FC, plus=max(c + 1, FC - 1)))
                        ins = pe.matmul((C, B)[half][:, s * P:(s + 1) * P], h_sb[:, c, tok], w2_sb[:, c],
                                        start=c == 0, stop=c == FC - 1)
                ins.then_inc(f2_done, 1)

            def o_back(t, r, half):
                pe.wait_ge(oT_copied, upto(t, r, 4, per=2, plus=half + 1))
                transposes(A, [oT_sb[:, half, k * P:(k + 1) * P] for k in range(4)]).then_inc(o_back_done, 1)

            def step(t, r):
                for u in range(UNITS):
                    if live(t, r, 2):
                        n, s = UNITS * (r - 2) + u, u // 2
                        tok = slice(s * P, (s + 1) * P)
                        if u == 0:
                            pe.wait_ge(stack_loaded[(r - 2) % 2], upto_dma(t, r, 2, per=STACK_DMAS * DMA))
                        if (v := upto(t, r, 2, per=UNITS, plus=u - 1)) is not None:
                            pe.wait_ge(max_done, v)
                        for j in range(HU):
                            h = HU * (u % 2) + j
                            ins = pe.matmul(s_ps[n % 2][:, j * P:(j + 1) * P], stack[0:PROD, (r - 2) % 4, 0, h, tok],
                                            stack[0:PROD, (r - 2) % 4, 1, h, tok], start=True, stop=True)
                        ins.then_inc(s_done, 1)
                    lag, unit = sT_unit(u)
                    if live(t, r, lag):
                        n, s = UNITS * (r - lag) + unit, unit // 2
                        tok = slice(s * P, (s + 1) * P)
                        if unit == 0:
                            pe.wait_ge(max_rows_loaded, upto(t, r, lag, per=MAXROWS * DMA, plus=MAXROWS * DMA))
                        if (v := upto(t, r, lag, per=UNITS, plus=unit - 1)) is not None:
                            pe.wait_ge(exp_done, v)
                        for j in range(HU):
                            h = HU * (unit % 2) + j
                            ins = pe.matmul(sT_ps[n % 2][:, j * P:(j + 1) * P], stack[:, (r - lag) % 4, 1, h, tok],
                                            stack[:, (r - lag) % 4, 0, h, tok], start=True, stop=True)
                        ins.then_inc(sT_done, 1)
                    if u == 0:
                        if live(t, r, 3):
                            pe.wait_ge(max_done, upto(t, r, 3, per=UNITS, plus=UNITS))
                            if (v := upto(t, r, 5, plus=1)) is not None:
                                pe.wait_ge(z_done, v)
                            pe.transpose(A[0:H * SEQS, 0:P], max_sb[:, (r - 3) % 2].rearrange("p h s -> p (h s)"),
                                         ident[:]).then_inc(maxT_done, 1)
                        if live(t, r, 6):
                            down(t, r, 6, 1)
                    if u == 1:
                        if live(t, r, 4):
                            if live(t, r, 3):
                                pe.wait_ge(max_rest_made, upto(t, r, 3, plus=1))
                            else:
                                pe.wait_ge(z_done, upto(t, r, 5, plus=1))
                            o_back(t, r, 0)
                        if live(t, r, 0):
                            pe.wait_ge(x_loaded[r % 2], upto_dma(t, r, 0))
                            if (v := upto(t, r, 6, per=2, plus=1)) is not None:
                                pe.wait_ge(y_done, v)
                            transposes(C, [x_sb[:, r % 2, s] for s in range(SEQS)]).then_inc(xT_done, 1)
                    if u == 2:
                        if live(t, r, 1):
                            pe.wait_ge(xT_joined, upto(t, r, 1, plus=1))
                            if live(t, r, 4):
                                pe.wait_ge(o_normed, upto(t, r, 4, per=2, plus=1))
                            elif live(t, r, 3):
                                pe.wait_ge(max_rest_made, upto(t, r, 3, plus=1))
                            else:
                                pe.wait_ge(rest_made, upto(t, r, 1, per=2, plus=2))
                            for s in range(SEQS):
                                ins = pe.matmul(A[:, s * P:(s + 1) * P], xT_sb[:, (r - 1) % 2, s * P:(s + 1) * P],
                                                wv_sb[:], start=True, stop=True)
                            ins.then_inc(v_done, 1)
                        if live(t, r, 5):
                            pe.wait_ge(n_done, upto(t, r, 5, plus=1))
                            pe.wait_ge(xT_lo, upto(t, r, 0, plus=1))
                            if not live(t, r, 0) and (v := upto(t, r, 6, per=2, plus=1)) is not None:
                                pe.wait_ge(y_done, v)
                            transposes(C, [n_sb[:, s] for s in range(SEQS)]).then_inc(nT_done, 1)
                        if live(t, r, 0):
                            if (v := upto(t, r, 6, per=2, plus=2)) is not None:
                                pe.wait_ge(y_done, v)
                            elif (v := upto(t, r, 0, per=2)) is not None:
                                pe.wait_ge(rest_made, v)
                            pe.wait_ge(xT_lo, upto(t, r, 0, plus=1))
                            three_products(B[:], wq_parts[:], xT_parts).then_inc(q_done, 1)
                    if u == 3:
                        if live(t, r, 0):
                            if (v := upto(t, r, 1, plus=1)) is not None:
                                pe.wait_ge(v_copied, v)
                            three_products(A[:], wk_parts[:], xT_parts).then_inc(k_done, 1)
                        if live(t, r, 5):
                            hidden(t, r, 0)
                    if u == 4:
                        if live(t, r, 5):
                            hidden(t, r, 1)
                        if live(t, r, 4):
                            pe.wait_ge(rest_made, upto(t, r, 0, per=2, plus=2))
                            if not live(t, r, 0):
                                pe.wait_ge(v_copied, upto(t, r, 1, plus=1))
                                pe.wait_ge(o_normed, upto(t, r, 4, per=2, plus=1))
                            o_back(t, r, 1)
                    if u == 5:
                        if live(t, r, 5):
                            hidden(t, r, 2)
                        if live(t, r, 4):
                            pe.wait_ge(o_normed, upto(t, r, 4, per=2, plus=2))
                            transposes(A, [o_sb[:, s] for s in range(SEQS)]).then_inc(onT_done, 1)
                    if u == 6:
                        if live(t, r, 5):
                            hidden(t, r, 3)
                        if live(t, r, 4):
                            pe.wait_ge(onT_copied, upto(t, r, 4, plus=1))
                            for s in range(SEQS):
                                ins = pe.matmul(A[:, s * P:(s + 1) * P], onT_sb[:, s * P:(s + 1) * P], wo_sb[:],
                                                start=True, stop=True)
                            ins.then_inc(wo_done, 1)
                    if u == 7 and live(t, r, 5):
                        down(t, r, 5, 0)
                    lag, unit = sT_unit(u)
                    if live(t, r, lag):
                        n, s = UNITS * (r - lag) + unit, unit // 2
                        pe.wait_ge(exp_done, upto(t, r, lag, per=UNITS, plus=unit + 1))
                        if unit == 0:
                            pe.wait_ge(v_copied, upto(t, r, lag, plus=1))
                        if unit % 4 == 0:
                            if (v := upto(t, r, lag, per=2, plus=unit // 4)) is not None:
                                pe.wait_ge(oT_copied, v)
                        for j in range(HU):
                            h = HU * (unit % 2) + j
                            ins = pe.matmul(oT_ps[j * VW:(j + 1) * VW, (unit % 4) * P:(unit % 4 + 1) * P],
                                            v_ones[:, (r - lag) % 4, s, h], prob_sb[:, n % 4, j * P:(j + 1) * P],
                                            start=True, stop=True)
                        ins.then_inc(pv_done, 1)

            step(0, 0)
            pe.wait_ge(consts_loaded, N_CONST * DMA)
            pe.wait_ge(consts_set, N_SET)
            pe.wait_ge(bv_wide_set, 1)
            for s in range(SEQS):
                ins = pe.matmul(s_ps[0][:, s * P:(s + 1) * P], bv_wide[:], wo_sb[:], start=True, stop=True)
            ins.then_inc(w_products_done, 1)
            for c in range(FC):
                ins = pe.matmul(s_ps[1][:, c:c + 1], w1_sb[:, c * P:(c + 1) * P], be1_col[:], start=True, stop=True)
            ins.then_inc(w_products_done, 1)
            step(0, 1)
            pe.wait_ge(consts_made, N_MADE)
            pe.wait_ge(stack_ones_set, 2)
            iterate(pe, step, 2, 2 * UNROLL, G, 6)


NAMES = ["wq", "bq", "wk", "bk", "wv", "bv", "wo", "bo", "w1", "b1", "w2", "b2", "ln1_g", "ln1_b", "ln2_g", "ln2_b"]


def kernel(**inputs):
    import numpy as _np
    import concourse.bacc as _bacc
    from concourse import mybir as _mybir
    from concourse.bass_utils import run_bass_kernel_spmd as _run

    nc = _bacc.Bacc("TRN2", target_bir_lowering=False, num_devices=1)
    arrays, args = {}, []
    for name in ["x"] + ["L0_conv_" + n for n in NAMES]:
        a = _np.ascontiguousarray(inputs[name])
        arrays[f"in_{name}"] = a
        args.append(nc.dram_tensor(f"in_{name}", a.shape, _mybir.dt.from_np(a.dtype), kind="ExternalInput").ap())
    out = nc.dram_tensor("out", arrays["in_x"].shape, F32, kind="ExternalOutput").ap()
    build(nc, *args, out)
    return _run(nc, [arrays], core_ids=[0]).results[0]["out"]
```
